# Optimizing a Trainium2 kernel written in Bass

```python
import numpy as np
import jax
import jax.numpy as jnp

def _softmax(x, axis=-1):
    return jax.nn.softmax(x, axis=axis)

def _gelu(x):
    return jax.nn.gelu(x, approximate=True)

def _silu(x):
    return jax.nn.silu(x)

def _sigmoid(x):
    return jax.nn.sigmoid(x)

def _layernorm(x, axis=-1, eps=1e-05):
    m = jnp.mean(x, axis=axis, keepdims=True)
    v = jnp.var(x, axis=axis, keepdims=True)
    return (x - m) / jnp.sqrt(v + eps)

def _scatter_add(tgt, idx, src, axis=0):
    return tgt.at[idx].add(src)

def _segment_sum(src, seg, n):
    return jax.ops.segment_sum(src, seg, n)
kernel_name = 'mk_seq_postln_d2_jaxref_r8_86c9fc'

def setup_inputs(seed: int=0):
    np.random.seed(seed)
    _w = jnp.asarray

    def _L0_attn_setup():
        import jax, jax.numpy as jnp
        import numpy as np
        E = 128
        H = 16
        D = E // H
        B = 2
        N = 1024
        CHUNK = 128
        LAYER_IDX = 0
        NUM_LAYERS = 12
        EPS = 1e-05

        def _build_slopes(n):

            def po2(m):
                start = 2.0 ** (-2.0 ** (-(np.log2(m) - 3)))
                return [start * start ** i for i in range(m)]
            if np.log2(n).is_integer():
                return po2(n)
            closest = 2 ** int(np.floor(np.log2(n)))
            return po2(closest) + _build_slopes(2 * closest)[0::2][:n - closest]

        def _slope_rate():
            s = np.array(_build_slopes(H), dtype=np.float32)
            s = s * (1.0 - LAYER_IDX / (NUM_LAYERS - 1) + 1e-05)
            return jnp.asarray(s)

        def lightning_attn(q, k, v, s):
            b, h, n, d = q.shape
            nc = n // CHUNK
            idx = jnp.arange(CHUNK, dtype=q.dtype)
            diff = idx[:, None] - idx[None, :]
            mask = jnp.where(diff >= 0, jnp.exp(-s[:, None, None] * diff), 0.0)
            lam_q = jnp.exp(-s[:, None] * (idx + 1.0))
            lam_k = jnp.exp(-s[:, None] * (CHUNK - 1.0 - idx))
            lam_c = jnp.exp(-s * CHUNK)

            def to_chunks(t):
                return t.reshape(b, h, nc, CHUNK, d).transpose(2, 0, 1, 3, 4)
            qc, kc, vc = (to_chunks(q), to_chunks(k), to_chunks(v))

            def step(kv, xs):
                qi, ki, vi = xs
                scores = jnp.einsum('bhid,bhjd->bhij', qi, ki) * mask
                o = jnp.einsum('bhij,bhjd->bhid', scores, vi)
                o = o + lam_q[:, :, None] * jnp.einsum('bhid,bhde->bhie', qi, kv)
                kv = lam_c[:, None, None] * kv + jnp.einsum('bhid,bhie->bhde', ki * lam_k[:, :, None], vi)
                return (kv, o)
            kv0 = jnp.zeros((b, h, d, d), q.dtype)
            _, o = jax.lax.scan(step, kv0, (qc, kc, vc))
            return o.transpose(1, 2, 0, 3, 4).reshape(b, h, n, d)
        key = jax.random.key(seed)
        ks = jax.random.split(key, 8)
        sc = 1.0 / np.sqrt(E)
        return {'x': jax.random.normal(ks[0], (B, N, E), jnp.float32), 'Wq': jax.random.normal(ks[1], (E, E), jnp.float32) * sc, 'Wk': jax.random.normal(ks[2], (E, E), jnp.float32) * sc, 'Wv': jax.random.normal(ks[3], (E, E), jnp.float32) * sc, 'Wo': jax.random.normal(ks[4], (E, E), jnp.float32) * sc, 'gamma': jnp.ones((E,), jnp.float32), 'beta': jnp.zeros((E,), jnp.float32), 'Wg1': jax.random.normal(ks[5], (E, D), jnp.float32) * sc, 'Wg2': jax.random.normal(ks[6], (D, E), jnp.float32) * (1.0 / np.sqrt(D))}
    _L0_attn_in = _L0_attn_setup()

    def _L0_ffn_setup():
        import jax, jax.numpy as jnp
        import numpy as np
        N_EXPERTS = 32
        TOP_K = 8
        N_GROUP = 4
        TOPK_GROUP = 2
        ROUTED_SCALING = 2.5

        def _gate(x, gate_w, gate_bias):
            T, E = (x.shape[0], gate_w.shape[0])
            logits = jnp.einsum('th,eh->te', x, gate_w)
            scores = jax.nn.sigmoid(logits)
            scores_choice = scores + gate_bias[None, :]
            grp = scores_choice.reshape(T, N_GROUP, E // N_GROUP)
            top2, _ = jax.lax.top_k(grp, 2)
            group_scores = top2.sum(-1)
            _, grp_idx = jax.lax.top_k(group_scores, TOPK_GROUP)
            group_mask = jax.nn.one_hot(grp_idx, N_GROUP, dtype=scores.dtype).sum(1)
            expert_mask = jnp.repeat(group_mask, E // N_GROUP, axis=1)
            masked = jnp.where(expert_mask > 0, scores_choice, 0.0)
            _, topk_idx = jax.lax.top_k(masked, TOP_K)
            topk_w = jnp.take_along_axis(scores, topk_idx, axis=1)
            topk_w = topk_w / (topk_w.sum(-1, keepdims=True) + 1e-20)
            topk_w = topk_w * ROUTED_SCALING
            return (topk_idx, topk_w)

        def _mlp(x, wg, wu, wd):
            return jnp.einsum('...i,hi->...h', jax.nn.silu(jnp.einsum('...h,ih->...i', x, wg)) * jnp.einsum('...h,ih->...i', x, wu), wd)
        key = jax.random.key(seed)
        ks = jax.random.split(key, 9)
        B, S, H, I = (2, 64, 128, 64)
        w = 0.02
        return {'hidden_states': jax.random.normal(ks[0], (B, S, H), jnp.float32), 'gate_w': jax.random.normal(ks[1], (N_EXPERTS, H), jnp.float32) * w, 'gate_bias': jax.random.normal(ks[2], (N_EXPERTS,), jnp.float32) * w, 'expert_gate': jax.random.normal(ks[3], (N_EXPERTS, I, H), jnp.float32) * w, 'expert_up': jax.random.normal(ks[4], (N_EXPERTS, I, H), jnp.float32) * w, 'expert_down': jax.random.normal(ks[5], (N_EXPERTS, H, I), jnp.float32) * w, 'shared_gate': jax.random.normal(ks[6], (2 * I, H), jnp.float32) * w, 'shared_up': jax.random.normal(ks[7], (2 * I, H), jnp.float32) * w, 'shared_down': jax.random.normal(ks[8], (H, 2 * I), jnp.float32) * w}
    _L0_ffn_in = _L0_ffn_setup()

    def _L1_attn_setup():
        import jax, jax.numpy as jnp
        import numpy as np
        B, T, D = (4, 512, 128)
        H, HD = (16, 64)
        EPS = 1e-06

        def _feature_map(x):
            return jax.nn.elu(x) + 1.0

        def _causal_linear_attention(q, k, v, eps=EPS):
            Dk = q.shape[-1]
            Dv = v.shape[-1]
            qT = jnp.moveaxis(q, 2, 0)
            kT = jnp.moveaxis(k, 2, 0)
            vT = jnp.moveaxis(v, 2, 0)
            S0 = jnp.zeros((q.shape[0], q.shape[1], Dk, Dv), dtype=q.dtype)
            z0 = jnp.zeros((q.shape[0], q.shape[1], Dk), dtype=q.dtype)

            def step(carry, qkv_t):
                S, z = carry
                q_t, k_t, v_t = qkv_t
                S = S + jnp.einsum('bhd,bhe->bhde', k_t, v_t)
                z = z + k_t
                num = jnp.einsum('bhd,bhde->bhe', q_t, S)
                den = jnp.einsum('bhd,bhd->bh', q_t, z) + eps
                return ((S, z), num / den[..., None])
            _, yT = jax.lax.scan(step, (S0, z0), (qT, kT, vT))
            return jnp.moveaxis(yT, 0, 2)
        key = jax.random.key(seed)
        ks = jax.random.split(key, 5)
        scale = 1.0 / np.sqrt(D)
        return {'x': jax.random.normal(ks[0], (B, T, D), dtype=jnp.float32), 'Wq': jax.random.normal(ks[1], (D, H * HD), dtype=jnp.float32) * scale, 'Wk': jax.random.normal(ks[2], (D, H * HD), dtype=jnp.float32) * scale, 'Wv': jax.random.normal(ks[3], (D, H * HD), dtype=jnp.float32) * scale, 'Wo': jax.random.normal(ks[4], (H * HD, D), dtype=jnp.float32) * scale}
    _L1_attn_in = _L1_attn_setup()

    def _L1_ffn_setup():
        import jax, jax.numpy as jnp
        import numpy as np
        E = 16
        K = 4
        NG = 4
        TG = 2
        SCALE = 2.5
        NORM_TOPK = True
        H = 128
        I = 64
        SH_I = I * 2
        B, S = (2, 256)
        key = jax.random.key(seed)
        ks = jax.random.split(key, 9)

        def w(k, shape, fan_in):
            return jax.random.normal(k, shape, jnp.float32) * (1.0 / np.sqrt(fan_in))
        return {'hidden_states': jax.random.normal(ks[0], (B, S, H), jnp.float32), 'gate_w': w(ks[1], (E, H), H), 'gate_bias': jnp.zeros((E,), jnp.float32), 'Wg': w(ks[2], (E, I, H), H), 'Wu': w(ks[3], (E, I, H), H), 'Wd': w(ks[4], (E, H, I), I), 'Ws_g': w(ks[5], (SH_I, H), H), 'Ws_u': w(ks[6], (SH_I, H), H), 'Ws_d': w(ks[7], (H, SH_I), SH_I)}
    _L1_ffn_in = _L1_ffn_setup()
    _d = {'L0_attn_x': _L0_attn_in['x'], 'L0_attn_Wq': _L0_attn_in['Wq'], 'L0_attn_Wk': _L0_attn_in['Wk'], 'L0_attn_Wv': _L0_attn_in['Wv'], 'L0_attn_Wo': _L0_attn_in['Wo'], 'L0_attn_gamma': _L0_attn_in['gamma'], 'L0_attn_beta': _L0_attn_in['beta'], 'L0_attn_Wg1': _L0_attn_in['Wg1'], 'L0_attn_Wg2': _L0_attn_in['Wg2'], 'L0_ffn_gate_w': _L0_ffn_in['gate_w'], 'L0_ffn_gate_bias': _L0_ffn_in['gate_bias'], 'L0_ffn_expert_gate': _L0_ffn_in['expert_gate'], 'L0_ffn_expert_up': _L0_ffn_in['expert_up'], 'L0_ffn_expert_down': _L0_ffn_in['expert_down'], 'L0_ffn_shared_gate': _L0_ffn_in['shared_gate'], 'L0_ffn_shared_up': _L0_ffn_in['shared_up'], 'L0_ffn_shared_down': _L0_ffn_in['shared_down'], 'L1_attn_Wq': _L1_attn_in['Wq'], 'L1_attn_Wk': _L1_attn_in['Wk'], 'L1_attn_Wv': _L1_attn_in['Wv'], 'L1_attn_Wo': _L1_attn_in['Wo'], 'L1_ffn_gate_w': _L1_ffn_in['gate_w'], 'L1_ffn_gate_bias': _L1_ffn_in['gate_bias'], 'L1_ffn_Wg': _L1_ffn_in['Wg'], 'L1_ffn_Wu': _L1_ffn_in['Wu'], 'L1_ffn_Wd': _L1_ffn_in['Wd'], 'L1_ffn_Ws_g': _L1_ffn_in['Ws_g'], 'L1_ffn_Ws_u': _L1_ffn_in['Ws_u'], 'L1_ffn_Ws_d': _L1_ffn_in['Ws_d']}
    _x0 = _d['L0_attn_x']
    _d['L0_attn_x'] = jax.random.normal(jax.random.fold_in(jax.random.key(seed), 1), (4, 1024, 128), dtype=_x0.dtype)
    del _x0
    return _d

def reference(L0_attn_x, L0_attn_Wq, L0_attn_Wk, L0_attn_Wv, L0_attn_Wo, L0_attn_gamma, L0_attn_beta, L0_attn_Wg1, L0_attn_Wg2, L0_ffn_gate_w, L0_ffn_gate_bias, L0_ffn_expert_gate, L0_ffn_expert_up, L0_ffn_expert_down, L0_ffn_shared_gate, L0_ffn_shared_up, L0_ffn_shared_down, L1_attn_Wq, L1_attn_Wk, L1_attn_Wv, L1_attn_Wo, L1_ffn_gate_w, L1_ffn_gate_bias, L1_ffn_Wg, L1_ffn_Wu, L1_ffn_Wd, L1_ffn_Ws_g, L1_ffn_Ws_u, L1_ffn_Ws_d):

    def _L0_attn_ref(x, Wq, Wk, Wv, Wo, gamma, beta, Wg1, Wg2):
        import jax, jax.numpy as jnp
        import numpy as np
        E = 128
        H = 16
        D = E // H
        B = 2
        N = 1024
        CHUNK = 128
        LAYER_IDX = 0
        NUM_LAYERS = 12
        EPS = 1e-05

        def _build_slopes(n):

            def po2(m):
                start = 2.0 ** (-2.0 ** (-(np.log2(m) - 3)))
                return [start * start ** i for i in range(m)]
            if np.log2(n).is_integer():
                return po2(n)
            closest = 2 ** int(np.floor(np.log2(n)))
            return po2(closest) + _build_slopes(2 * closest)[0::2][:n - closest]

        def _slope_rate():
            s = np.array(_build_slopes(H), dtype=np.float32)
            s = s * (1.0 - LAYER_IDX / (NUM_LAYERS - 1) + 1e-05)
            return jnp.asarray(s)

        def lightning_attn(q, k, v, s):
            b, h, n, d = q.shape
            nc = n // CHUNK
            idx = jnp.arange(CHUNK, dtype=q.dtype)
            diff = idx[:, None] - idx[None, :]
            mask = jnp.where(diff >= 0, jnp.exp(-s[:, None, None] * diff), 0.0)
            lam_q = jnp.exp(-s[:, None] * (idx + 1.0))
            lam_k = jnp.exp(-s[:, None] * (CHUNK - 1.0 - idx))
            lam_c = jnp.exp(-s * CHUNK)

            def to_chunks(t):
                return t.reshape(b, h, nc, CHUNK, d).transpose(2, 0, 1, 3, 4)
            qc, kc, vc = (to_chunks(q), to_chunks(k), to_chunks(v))

            def step(kv, xs):
                qi, ki, vi = xs
                scores = jnp.einsum('bhid,bhjd->bhij', qi, ki) * mask
                o = jnp.einsum('bhij,bhjd->bhid', scores, vi)
                o = o + lam_q[:, :, None] * jnp.einsum('bhid,bhde->bhie', qi, kv)
                kv = lam_c[:, None, None] * kv + jnp.einsum('bhid,bhie->bhde', ki * lam_k[:, :, None], vi)
                return (kv, o)
            kv0 = jnp.zeros((b, h, d, d), q.dtype)
            _, o = jax.lax.scan(step, kv0, (qc, kc, vc))
            return o.transpose(1, 2, 0, 3, 4).reshape(b, h, n, d)
        b, n, e = x.shape
        s = _slope_rate()
        silu = jax.nn.silu
        q = silu(x @ Wq)
        k = silu(x @ Wk)
        v = silu(x @ Wv)
        split = lambda t: t.reshape(b, n, H, D).transpose(0, 2, 1, 3)
        o = lightning_attn(split(q), split(k), split(v), s)
        o = o.transpose(0, 2, 1, 3).reshape(b, n, e)
        mu = jnp.mean(o, axis=-1, keepdims=True)
        var = jnp.var(o, axis=-1, keepdims=True)
        o = (o - mu) * jax.lax.rsqrt(var + EPS) * gamma + beta
        gate = jax.nn.sigmoid(x @ Wg1 @ Wg2)
        return o * gate @ Wo

    def _L0_ffn_ref(hidden_states, gate_w, gate_bias, expert_gate, expert_up, expert_down, shared_gate, shared_up, shared_down):
        import jax, jax.numpy as jnp
        import numpy as np
        N_EXPERTS = 32
        TOP_K = 8
        N_GROUP = 4
        TOPK_GROUP = 2
        ROUTED_SCALING = 2.5

        def _gate(x, gate_w, gate_bias):
            T, E = (x.shape[0], gate_w.shape[0])
            logits = jnp.einsum('th,eh->te', x, gate_w)
            scores = jax.nn.sigmoid(logits)
            scores_choice = scores + gate_bias[None, :]
            grp = scores_choice.reshape(T, N_GROUP, E // N_GROUP)
            top2, _ = jax.lax.top_k(grp, 2)
            group_scores = top2.sum(-1)
            _, grp_idx = jax.lax.top_k(group_scores, TOPK_GROUP)
            group_mask = jax.nn.one_hot(grp_idx, N_GROUP, dtype=scores.dtype).sum(1)
            expert_mask = jnp.repeat(group_mask, E // N_GROUP, axis=1)
            masked = jnp.where(expert_mask > 0, scores_choice, 0.0)
            _, topk_idx = jax.lax.top_k(masked, TOP_K)
            topk_w = jnp.take_along_axis(scores, topk_idx, axis=1)
            topk_w = topk_w / (topk_w.sum(-1, keepdims=True) + 1e-20)
            topk_w = topk_w * ROUTED_SCALING
            return (topk_idx, topk_w)

        def _mlp(x, wg, wu, wd):
            return jnp.einsum('...i,hi->...h', jax.nn.silu(jnp.einsum('...h,ih->...i', x, wg)) * jnp.einsum('...h,ih->...i', x, wu), wd)
        orig_shape = hidden_states.shape
        H = orig_shape[-1]
        residuals = hidden_states
        x = hidden_states.reshape(-1, H)
        topk_idx, topk_w = _gate(x, gate_w, gate_bias)
        g = jnp.einsum('th,eih->eti', x, expert_gate)
        u = jnp.einsum('th,eih->eti', x, expert_up)
        outs = jnp.einsum('eti,ehi->eth', jax.nn.silu(g) * u, expert_down)
        outs_t = jnp.transpose(outs, (1, 0, 2))
        gathered = jnp.take_along_axis(outs_t, topk_idx[:, :, None], axis=1)
        final = (gathered * topk_w[:, :, None]).sum(1)
        shared = _mlp(residuals, shared_gate, shared_up, shared_down)
        return final.reshape(orig_shape) + shared

    def _L1_attn_ref(x, Wq, Wk, Wv, Wo):
        import jax, jax.numpy as jnp
        import numpy as np
        B, T, D = (4, 512, 128)
        H, HD = (16, 64)
        EPS = 1e-06

        def _feature_map(x):
            return jax.nn.elu(x) + 1.0

        def _causal_linear_attention(q, k, v, eps=EPS):
            Dk = q.shape[-1]
            Dv = v.shape[-1]
            qT = jnp.moveaxis(q, 2, 0)
            kT = jnp.moveaxis(k, 2, 0)
            vT = jnp.moveaxis(v, 2, 0)
            S0 = jnp.zeros((q.shape[0], q.shape[1], Dk, Dv), dtype=q.dtype)
            z0 = jnp.zeros((q.shape[0], q.shape[1], Dk), dtype=q.dtype)

            def step(carry, qkv_t):
                S, z = carry
                q_t, k_t, v_t = qkv_t
                S = S + jnp.einsum('bhd,bhe->bhde', k_t, v_t)
                z = z + k_t
                num = jnp.einsum('bhd,bhde->bhe', q_t, S)
                den = jnp.einsum('bhd,bhd->bh', q_t, z) + eps
                return ((S, z), num / den[..., None])
            _, yT = jax.lax.scan(step, (S0, z0), (qT, kT, vT))
            return jnp.moveaxis(yT, 0, 2)
        b, t, _ = x.shape

        def proj(W):
            return (x @ W).reshape(b, t, H, HD).transpose(0, 2, 1, 3)
        q = _feature_map(proj(Wq))
        k = _feature_map(proj(Wk))
        v = proj(Wv)
        y = _causal_linear_attention(q, k, v)
        y = y.transpose(0, 2, 1, 3).reshape(b, t, H * HD)
        return y @ Wo

    def _L1_ffn_ref(hidden_states, gate_w, gate_bias, Wg, Wu, Wd, Ws_g, Ws_u, Ws_d):
        import jax, jax.numpy as jnp
        import numpy as np
        E = 16
        K = 4
        NG = 4
        TG = 2
        SCALE = 2.5
        NORM_TOPK = True
        H = 128
        I = 64
        SH_I = I * 2
        B, S = (2, 256)
        x = hidden_states
        b, s, h = x.shape
        n = b * s
        xf = x.reshape(n, h)
        logits = xf @ gate_w.T
        scores = jax.nn.sigmoid(logits)
        sfc = scores + gate_bias
        epg = E // NG
        grp = sfc.reshape(n, NG, epg)
        g_scores = jax.lax.top_k(grp, 2)[0].sum(-1)
        _, gidx = jax.lax.top_k(g_scores, TG)
        gmask = jax.nn.one_hot(gidx, NG, dtype=sfc.dtype).sum(1)
        emask = jnp.repeat(gmask, epg, axis=1)
        masked = jnp.where(emask > 0, sfc, -jnp.inf)
        _, topk_idx = jax.lax.top_k(masked, K)
        topk_w = jnp.take_along_axis(scores, topk_idx, axis=1)
        if K > 1 and NORM_TOPK:
            topk_w = topk_w / (topk_w.sum(-1, keepdims=True) + 1e-20)
        topk_w = topk_w * SCALE
        cw = (jax.nn.one_hot(topk_idx, E, dtype=topk_w.dtype) * topk_w[..., None]).sum(1)
        hg = jnp.einsum('nh,eih->nei', xf, Wg)
        hu = jnp.einsum('nh,eih->nei', xf, Wu)
        act = jax.nn.silu(hg) * hu
        y = jnp.einsum('nei,ne,ehi->nh', act, cw, Wd)
        shared = jax.nn.silu(xf @ Ws_g.T) * (xf @ Ws_u.T) @ Ws_d.T
        y = y + shared
        return (x + y.reshape(b, s, h)).astype(hidden_states.dtype)
    x = L0_attn_x
    x = _layernorm(x + _L0_attn_ref(x, L0_attn_Wq, L0_attn_Wk, L0_attn_Wv, L0_attn_Wo, L0_attn_gamma, L0_attn_beta, L0_attn_Wg1, L0_attn_Wg2), axis=-1)
    x = _layernorm(x + _L0_ffn_ref(x, L0_ffn_gate_w, L0_ffn_gate_bias, L0_ffn_expert_gate, L0_ffn_expert_up, L0_ffn_expert_down, L0_ffn_shared_gate, L0_ffn_shared_up, L0_ffn_shared_down), axis=-1)
    x = _layernorm(x + _L1_attn_ref(x, L1_attn_Wq, L1_attn_Wk, L1_attn_Wv, L1_attn_Wo), axis=-1)
    x = _layernorm(x + _L1_ffn_ref(x, L1_ffn_gate_w, L1_ffn_gate_bias, L1_ffn_Wg, L1_ffn_Wu, L1_ffn_Wd, L1_ffn_Ws_g, L1_ffn_Ws_u, L1_ffn_Ws_d), axis=-1)
    return x

_drawn_inputs = setup_inputs


def setup_inputs(seed=0):
    import zlib

    import numpy as np

    out = dict(_drawn_inputs(seed))
    spreads = {'L0_attn_gamma': (1.0, 0.2), 'L0_attn_beta': (0.0, 0.1), 'L1_ffn_gate_bias': (0.0, 0.1)}
    factors = {'L0_ffn_gate_w': 3.066,
     'L0_ffn_gate_bias': 3.814,
     'L0_ffn_expert_gate': 3.379,
     'L0_ffn_expert_up': 3.001,
     'L0_ffn_expert_down': 3.231}
    for name, (base, spread) in spreads.items():
        noise = np.random.default_rng([zlib.crc32(name.encode()), seed]).standard_normal(out[name].shape)
        drawn = base * np.exp(spread * noise) if base else spread * noise
        out[name] = jnp.asarray(drawn.astype(out[name].dtype))
    for name, factor in factors.items():
        out[name] = (out[name] * factor).astype(out[name].dtype)
    return out
```

```python
from contextlib import ExitStack

import numpy as np

import concourse.bass as bass
from concourse import mybir

F32 = mybir.dt.float32
BF16 = mybir.dt.bfloat16
ALU = mybir.AluOpType
ACT = mybir.ActivationFunctionType
AX = mybir.AxisListType

P = 128
E = 128
BATCH, SEQ = 4, 1024
TOK = BATCH * SEQ
GROUP = 512
NG = TOK // GROUP
CH = 128
NC = GROUP // CH
H0, D0 = 16, 8
H2, D2 = 16, 64
PAIRS = H2 // 2
EXPERTS = (32, 16)
INNER = 64
NPAIR = tuple(n // 2 for n in EXPERTS)
RW = 32
RG = 4
PAD = -2e30
OUT_OF_GROUP = 1e30
TAKEN = -3e38
SCALE = 2.5

C_MASK0 = 0
C_LAMQ = C_MASK0 + H0 * CH
C_LAMK = C_LAMQ + CH
C_BLOCK = C_LAMK + E
C_TRI = C_BLOCK + E
C_IDENT = C_TRI + CH
C_MEAN = C_IDENT + P
C_HEAD = C_MEAN + P
C_LOWER = C_HEAD + 4
C_UPPER = C_LOWER + RG * RG
C_LAMC = C_UPPER + RG * RG
C_EPS = C_LAMC + 1
C_HALF = C_EPS + 1
C_END = C_HALF + 2

ORDER2 = [("q", p) for p in range(PAIRS)] + [("kv", 0), ("kT", 0)]
for _c in range(NC):
    ORDER2.append(("sc", _c))
    if _c:
        ORDER2.append(("yT", _c - 1))
    if _c + 1 < NC:
        ORDER2.append(("kv", _c + 1))
    ORDER2 += [("num", _c), ("U", _c)]
    if _c + 1 < NC:
        ORDER2.append(("kT", _c + 1))
ORDER2 += [("yT", NC - 1), ("wo", 0)]
FILLS = {"q": 1, "kv": 4, "kT": 2, "sc": 4, "U": 3, "yT": 2, "num": 0, "wo": 0}
FIRST, RING_JOBS = {}, []
for _s in ORDER2:
    FIRST[_s] = len(RING_JOBS)
    RING_JOBS += [(*_s, m) for m in range(FILLS[_s[0]])]
RING = 4
JOBS = len(RING_JOBS)
assert JOBS % RING == 0
ORDER0 = ["q", "k", "g1", "kv01", "gate", "kv23"] + [(s, c) for c in range(NC) for s in ("sc", "pv")]
UPAIRS = ((0, 3), (3, 6), (6, 8))
NORM_STEPS = 8
ROUTE_STEPS = 5
ATTN_NORM_STEPS = 9
ROUTE_OPS = (23, 26)
TAIL_STEPS = (ATTN_NORM_STEPS + NORM_STEPS + ROUTE_STEPS, NORM_STEPS, NORM_STEPS + ROUTE_STEPS, NORM_STEPS)
MAIN_HOOKS = (len(ORDER0), NPAIR[0] + 1, len(ORDER2), NPAIR[1] + 1)


def emptied(job):
    step, c, m = job
    if step == "q":
        return "er", 16, c + 1
    if step == "kv":
        return ("er", 16, 8 + 2 * c + m + 1) if m < 2 else ("v", 8, 2 * c + m - 1)
    return {"kT": ("kT", 8, 2 * c + m + 1), "sc": ("mask", 16, 4 * c + m + 1),
            "U": ("add", 12, 3 * c + m + 1), "yT": ("yT", 8, 2 * c + m + 1)}[step]


def schedule(eng, main, tail):
    def hooked(stage, prev_stage, prev_g, prev_parity):
        n, steps = MAIN_HOOKS[stage], TAIL_STEPS[prev_stage]

        def hook(i):
            for k in range(i * steps // n, (i + 1) * steps // n):
                tail(prev_stage, prev_g, prev_parity, k)
        return hook

    for stage in range(4):
        if stage:
            main(stage, 0, 0, hooked(stage, stage - 1, NG - 1, 1))
        else:
            main(stage, 0, 0, lambda i: None)
        main(stage, 1, 1, hooked(stage, stage, 0, 0))
        with eng.Fori(0, (NG - 2) // 2) as b:
            main(stage, b * 2 + 2, 0, hooked(stage, stage, b * 2 + 1, 1))
            main(stage, b * 2 + 3, 1, hooked(stage, stage, b * 2 + 2, 0))
    for k in range(TAIL_STEPS[3]):
        tail(3, NG - 1, 1, k)


def last_use(s, n, m):
    return s - m if s >= m else max(t for t in range(n) if t % m == s % m) - n


def wait(eng, sem, value):
    if not isinstance(value, int) or value > 0:
        eng.wait_ge(sem, value)


def wait_apart(eng, sem, value, passed):
    if isinstance(value, int):
        wait(eng, sem, value)
    else:
        eng.wait_ge(sem, value)
        eng.sem_inc(passed, 1)


def build(nc, a, out):
    with ExitStack() as ctx:
        def sb(name, shape, dt=F32):
            return ctx.enter_context(nc.sbuf_tensor(name, shape, dt))

        def sem(name):
            return ctx.enter_context(nc.semaphore(name))

        bank = [ctx.enter_context(nc.psum_tensor(f"bank{i}", [P, GROUP], F32)) for i in range(8)]
        T = bank[7]
        T16 = T[:].bitcast(BF16)
        cst = sb("cst", [P, C_END])
        XT = sb("XT", [P, TOK])
        xg = sb("xg", [P, 2, GROUP])
        w0 = sb("w0", [P, 6, E])
        gb = sb("gb", [P, 2])
        w_gu = [sb("w_gu", [P, NPAIR[0] + 1, 2, E])]
        w_dn = [sb("w_dn", [P, NPAIR[0] + 1, E])]
        w_gu.append(w_gu[0][:, 0:NPAIR[1] + 1, :, :])
        w_dn.append(w_dn[0][:, 0:NPAIR[1] + 1, :])
        w2 = sb("w2", [P, 3, H2 * D2])
        w2o = sb("w2o", [P, PAIRS, E])
        w_route = [sb(f"w_route{i}", [P, EXPERTS[i]]) for i in range(2)]
        rbias = [sb(f"rbias{i}", [P, RW]) for i in range(2)]
        ident16 = sb("ident16", [P, P], BF16)
        sel = [sb(f"sel{i}", [96, NPAIR[i], P], BF16) for i in range(2)]
        CW = sb("CW", [96, TOK], BF16)
        probs = sb("probs", [P, 2, 16, CH])
        arena1 = sb("arena1", [P, 4096])
        arena2 = sb("arena2", [P, 4096])
        arena3 = sb("arena3", [P, 4096])
        arena4 = sb("arena4", [P, 1024])
        sig = arena3[:, 0:1024].rearrange("p (b t) -> p b t", b=2)
        qT = arena3[:, 1024:1536].rearrange("p (c t) -> p c t", c=NC)
        kz = arena1[:, 0:2048].rearrange("p (q t) -> p q t", q=4)
        qbd = arena1[:, 2048:4096].rearrange("p (c r t) -> p c r t", c=NC, r=4)
        vpad = arena2[:, :].rearrange("p (b h e) -> p b h e", b=2, h=H0)
        qs = arena3[:, 1536:2048].rearrange("p (c t) -> p c t", c=NC)
        ks = arena3[:, 2048:2560].rearrange("p (c t) -> p c t", c=NC)
        KV = arena3[:, 2560:3584].rearrange("p (c k t) -> p c k t", c=NC, k=2)
        g1 = arena3[:, 3584:4096]
        gate = sb("gate", [P, 2, GROUP])
        S0 = sb("S0", [P, E])
        upd = sb("upd", [P, E])
        o = arena4[:, 0:GROUP]
        og = arena4[:, GROUP:2 * GROUP]
        fs = sb("fs", [P, 2, GROUP])
        ft = sb("ft", [P, 2, GROUP])
        fh = sb("fh", [P, 3, GROUP])
        q2 = arena1[:, :].rearrange("p (r t) -> p r t", r=PAIRS)
        yT2 = arena2[:, :].rearrange("p (r t) -> p r t", r=PAIRS)
        relu2 = fs
        exp2 = ft
        k2 = cst[:, C_MASK0:C_LAMQ].rearrange("p (b t) -> p b t", b=2)
        v2 = sb("v2", [P, 2, H2, D2 + 1])
        kT2 = arena4[:, :].rearrange("p (r t) -> p r t", r=PAIRS)
        qb2 = arena3[:, :].rearrange("p (b r h t) -> p b r h t", b=2, r=PAIRS, h=2)
        S2 = sb("S2", [P, PAIRS, 2 * (D2 + 1)])
        den2 = sb("den2", [P, 2, H2])
        y2 = fh[:, 0:2, :].rearrange("p b (h d) -> p (b h) d", d=D2)
        r = sb("r", [P, GROUP])
        c_ = r
        sq = sb("sq", [P, GROUP])
        std = sb("std", [P, GROUP])
        rs = std
        xo = sb("xo", [P, GROUP])
        sg = [sb(f"sg{i}", [P, NC, RG, 8]) for i in range(2)]
        ch = sb("ch", [P, NC * RG, 8])
        top8 = sb("top8", [P, NC * RG, 8])
        gs = sb("gs", [P, NC, RG])
        ge = sb("ge", [P, NC, RG, RG])
        gt = sb("gt", [P, NC, RG, RG])
        rank = sb("rank", [P, NC * RG])
        fill = sb("fill", [P, NC * RG])
        top = sb("top", [P, NC, 8])
        mr = sb("mr", [P, NC, RW])
        wsum = sb("wsum", [P, NC])
        cw = sb("cw", [P, NC, RW])
        parts = sb("parts", [P, NC, 3, RW], BF16)

        mask0 = cst[:, C_MASK0:C_LAMQ].rearrange("p (h t) -> p h t", h=H0)
        lamq = cst[:, C_LAMQ:C_LAMK]
        lamk = cst[:, C_LAMK:C_BLOCK]
        block0 = cst[:, C_BLOCK:C_TRI]
        tri = cst[:, C_TRI:C_IDENT]
        ident = cst[:, C_IDENT:C_MEAN]
        mean_w = cst[:, C_MEAN:C_HEAD]
        lower = cst[:, C_LOWER:C_UPPER].rearrange("p (i j) -> p i j", i=RG)
        upper = cst[:, C_UPPER:C_LAMC].rearrange("p (i j) -> p i j", i=RG)
        lamc = cst[:, C_LAMC:C_LAMC + 1]
        eps = cst[:, C_EPS:C_EPS + 1]

        d_x0, d_x = sem("x_group0_loaded"), sem("x_rest_loaded")
        d_cst, d_w0, d_sel = sem("constants_loaded"), sem("stage0_weights_loaded"), sem("selectors_loaded")
        d_w13 = [sem("stage1_weights_loaded"), sem("stage3_weights_loaded")]
        d_w2 = sem("stage2_weights_loaded")
        d_out = sem("output_stored")
        init_pool, init_dve = sem("pool_init_done"), sem("selectors_ready")
        passed_pool, passed_dve = sem("passed_pool"), sem("passed_dve")
        init_v, init_s2 = sem("stage0_buffers_zeroed"), sem("stage2_buffers_set")
        xg_ready = sem("xg_ready")
        a_proj = sem("a_projection_ready")
        a_sig = sem("a_sigmoid_ready")
        a_g1 = sem("a_g1_ready")
        a_gate = sem("a_gate_ready")
        a_q, a_k, a_kv = sem("a_q_ready"), sem("a_k_ready"), sem("a_kv_ready")
        a_qbd = sem("a_qbd_ready")
        a_qs, a_ks, a_v = sem("a_qscaled_ready"), sem("a_kscaled_ready"), sem("a_vpad_ready")
        a_score, a_mask = sem("a_scores_ready"), sem("a_masked_ready")
        a_upd, a_updr, a_state = sem("a_update_ready"), sem("a_update_read"), sem("a_state_ready")
        a_attn = sem("a_attention_ready")
        a_o, a_mean, a_c, a_sq, a_var, a_std = (sem("a_norm_" + n) for n in ("o", "mean", "c", "sq", "var", "std"))
        a_rs, a_n, a_gb, a_og = (sem("a_norm_" + n) for n in ("rs", "n", "gb", "og"))
        f_g, f_u, f_w = ([sem(f"f{i}_{n}_ready") for i in (1, 3)] for n in ("gate", "up", "weight"))
        f_s, f_t, f_h = ([sem(f"f{i}_{n}_ready") for i in (1, 3)] for n in ("silu", "su", "hidden"))
        f_d = [sem(f"f{i}_down_done") for i in (1, 3)]
        c_filled = sem("c_ring_filled")
        c_er = sem("c_relu_exp_ready")
        c_comb = sem("c_features_ready")
        c_v, c_yT = sem("c_v_ready"), sem("c_yT_ready")
        c_kT, c_mask = sem("c_kT_ready"), sem("c_masked_ready")
        c_qb = sem("c_qbd_ready")
        c_num, c_y, c_add = sem("c_numerator_ready"), sem("c_y_ready"), sem("c_state_added")
        c_empty = {"er": c_er, "v": c_v, "kT": c_kT, "mask": c_mask, "add": c_add, "yT": c_yT}
        c_den = sem("c_denominator_step")
        a_y, c_y_out = sem("a_output_ready"), sem("c_output_ready")
        t_r, t_mean, t_c, t_sq, t_var, t_std, t_rs, t_xo = (
            sem("t_" + n) for n in ("residual", "mean", "centred", "square", "variance", "std", "rstd", "xo"))
        xt_ready = sem("xt_ready")
        t_logit, t_sig, t_cwp, t_cwt, t_cw = (
            sem("t_" + n) for n in ("logits", "scores", "weight_parts", "weights_transposed", "weights"))
        route_step = sem("route_step")

        block = ctx.enter_context(nc.Block())

        def cols(g):
            return bass.ds(g * GROUP, GROUP)

        def tails(stage, g):
            return g + NG * stage

        def routes(stage, g):
            return g + NG * (stage // 2)

        @block.sync
        def _(sp):
            sp.dma_start(cst[:, :], a["cst"]).then_inc(d_cst, 16)
            sp.dma_start(XT[:, 0:GROUP], a["x"][:, 0:GROUP]).then_inc(d_x0, 16)
            for i, n in enumerate(("Wq", "Wk", "Wv", None, None, "Wo")):
                if n:
                    sp.dma_start(w0[:, i, :], a["a" + n]).then_inc(d_w0, 16)
            sp.wait_ge(init_pool, 2)
            sp.dma_start(w0[:, 3, 0:D0], a["aWg1"]).then_inc(d_w0, 16)
            sp.dma_start(w0[0:D0, 4, :], a["aWg2"]).then_inc(d_w0, 16)
            sp.dma_start(gb[:, 0:1], a["gamma"]).then_inc(d_w0, 16)
            sp.dma_start(gb[:, 1:2], a["beta"]).then_inc(d_w0, 16)
            sp.dma_start(w_route[0][:, :], a["gw1"]).then_inc(d_w0, 16)
            sp.dma_start(rbias[0][:, :], a["gb1"]).then_inc(d_w0, 16)
            sp.dma_start(XT[:, GROUP:TOK], a["x"][:, GROUP:TOK]).then_inc(d_x, 16)
            sel_stage = probs[0:96, :, :, :].rearrange("p a b c -> p (a b c)")
            sp.dma_start(sel_stage[:, 0:(NPAIR[0] + NPAIR[1]) * P], a["sel"]).then_inc(d_sel, 16)
            for i in range(2):
                n = NPAIR[i]
                gu, dn = a[f"gu{i}"], a[f"dn{i}"]
                if i == 1:
                    sp.wait_ge(f_d[0], NG * (NPAIR[0] + 1))
                sp.dma_start(w_gu[i][:, :, :, :], gu).then_inc(d_w13[i], 16)
                sp.dma_start(w_dn[i][:, :, :], dn).then_inc(d_w13[i], 16)
                if i == 0:
                    sp.dma_start(w2[:, :, :], a["w2"]).then_inc(d_w2, 16)
                    sp.dma_start(w2o[:, :, :], a["w2o"]).then_inc(d_w2, 16)
                    sp.dma_start(w_route[1][:, :], a["gw3"]).then_inc(d_w2, 16)
                    sp.dma_start(rbias[1][:, :].rearrange("p (g k) -> p g k", g=RG)[:, :, 0:4],
                                 a["gb3"].rearrange("p (g k) -> p g k", g=RG)).then_inc(d_w2, 16)
            for g in range(NG):
                sp.wait_ge(xt_ready, 3 * NG + g + 1)
                sp.dma_start(out[:, g * GROUP:(g + 1) * GROUP], XT[:, g * GROUP:(g + 1) * GROUP]).then_inc(d_out, 16)
            sp.wait_ge(d_out, 16 * NG)

        @block.tensor
        def _(pe):
            def main0(g, par, hook):
                x = xg[:, par, :]
                for i, step in enumerate(ORDER0):
                    hook(i)
                    if step == "q":
                        if isinstance(g, int) and g == 0:
                            pe.wait_ge(d_w0, 16 * 10)
                            pe.wait_ge(init_v, 3)
                        pe.wait_ge(xg_ready, g + 1)
                        wait(pe, a_mask, g * 16)
                        pe.matmul(bank[0][:, :], w0[:, 0, :], x, start=True, stop=True).then_inc(a_proj, 1)
                    elif step == "k":
                        pe.matmul(bank[1][:, :], w0[:, 1, :], x, start=True, stop=True).then_inc(a_proj, 1)
                    elif step == "g1":
                        pe.matmul(bank[2][:, :], w0[:, 3, :], x, start=True, stop=True).then_inc(a_proj, 1)
                    elif step in ("kv01", "kv23"):
                        b, c0 = (bank[3], 0) if step == "kv01" else (bank[0], 2)
                        if step == "kv23":
                            pe.wait_ge(a_q, g + 1)
                        for c in (c0, c0 + 1):
                            last = pe.matmul(b[:, (c - c0) * 2 * E:(c - c0 + 1) * 2 * E],
                                             x[:, c * CH:(c + 1) * CH], w0[:, 1:3, :], start=True, stop=True)
                        last.then_inc(a_proj, 1)
                    elif step == "gate":
                        pe.wait_ge(a_g1, g + 1)
                        pe.matmul(bank[2][:, :], w0[:, 4, :], g1[:, :], start=True, stop=True).then_inc(a_proj, 1)
                    elif step[0] == "sc":
                        c = step[1]
                        n = g * NC + c
                        if c == 0:
                            pe.wait_ge(a_k, g + 1)
                            pe.wait_ge(a_qbd, g + 1)
                            pe.wait_ge(a_kv, g * 2 + 2)
                            pe.wait_ge(a_gate, g + 1)
                        for s in range(4):
                            if c:
                                pe.wait_ge(a_mask, n * 4 - 3 + s)
                            pe.matmul(bank[s][:, :], kz[:, s, c * CH:(c + 1) * CH],
                                      qbd[:, c, :, :], start=True, stop=True).then_inc(a_score, 1)
                    else:
                        c = step[1]
                        n = g * NC + c
                        if c == 0:
                            pe.wait_ge(a_ks, g + 1)
                            pe.wait_ge(a_qs, g + 1)
                        wait(pe, a_updr, n)
                        pe.matmul(bank[5][:, 0:E], ks[:, c, :], KV[:, c, 1, :], start=True, stop=True).then_inc(a_upd, 1)
                        wait(pe, a_state, n)
                        if c == 0:
                            wait(pe, a_o, g)
                        oc = bank[4][:, c * CH:(c + 1) * CH]
                        pe.matmul(oc, S0[:, :], qs[:, c, :], start=True, stop=False)
                        pe.wait_ge(a_v, n + 1)
                        pe.wait_ge(a_mask, n * 4 + 4)
                        for h in range(H0):
                            last = pe.matmul(oc, vpad[:, c % 2, h, :], probs[:, c % 2, h, :],
                                             start=False, stop=(h == H0 - 1))
                        last.then_inc(a_attn, 1)

            def main13(i, g, par, hook):
                n_pairs, stage = NPAIR[i], 1 + 2 * i
                n = n_pairs + 1
                x = xg[:, par, :]

                def down(s):
                    if s < n_pairs:
                        pe.wait_ge(f_h[i], g * n_pairs + s + 1)
                    else:
                        pe.wait_ge(f_t[i], g * n + n)
                    if s == 0 and not (isinstance(g, int) and g == 0):
                        pe.wait_ge(t_r, NG * stage + g)
                    pe.matmul(bank[6][:, :], w_dn[i][:, s, :], fh[:, s % 3, :],
                              start=(s == 0), stop=(s == n_pairs)).then_inc(f_d[i], 1)

                for s in range(n):
                    hook(s)
                    if s == 0:
                        if isinstance(g, int) and g == 0:
                            pe.wait_ge(d_w13[i], 32)
                            if i == 0:
                                pe.wait_ge(init_dve, 3)
                                pe.wait_ge(a_mask, NG * NC * 4)
                                pe.wait_ge(a_o, NG)
                                pe.wait_ge(a_updr, NG * NC)
                            else:
                                pe.wait_ge(c_yT, NG * 8)
                                pe.wait_ge(c_add, NG * 12)
                                pe.wait_ge(c_mask, NG * 16)
                                pe.wait_ge(c_y, NG * NC)
                                pe.wait_ge(t_r, NG * 3)
                        pe.wait_ge(xg_ready, NG * stage + g + 1)
                    wait(pe, f_s[i], g * n + last_use(s, n, 2) + 1)
                    wait(pe, f_t[i], g * n + last_use(s, n, 2) + 1)
                    pe.matmul(bank[s % 2][:, :], w_gu[i][:, s, 0, :], x, start=True, stop=True).then_inc(f_g[i], 1)
                    pe.matmul(bank[2 + s % 2][:, :], w_gu[i][:, s, 1, :], x, start=True, stop=True).then_inc(f_u[i], 1)
                    if s < n_pairs:
                        if s == 0:
                            pe.wait_ge(t_cw, NG * i + g + 1)
                        wait(pe, f_h[i], g * n_pairs + last_use(s, n_pairs, 2) + 1)
                        pe.matmul(bank[4 + s % 2][:, :], sel[i][:, s, :], CW[:, cols(g)],
                                  start=True, stop=True).then_inc(f_w[i], 1)
                    if s >= 2:
                        down(s - 2)
                down(n - 2)
                down(n - 1)

            def main2(g, par, hook):
                x = xg[:, par, :]

                def ring_wait(j):
                    k = j - RING
                    name, per_group, count = emptied(RING_JOBS[k])
                    wait(pe, c_empty[name], (g if k >= 0 else g - 1) * per_group + count)

                for i, (step, c) in enumerate(ORDER2):
                    hook(i)
                    j = FIRST[(step, c)]
                    n = g * NC + c
                    if i == 0:
                        if isinstance(g, int) and g == 0:
                            pe.wait_ge(d_w2, 64)
                            pe.wait_ge(init_s2, 3)
                            pe.wait_ge(f_s[0], NG * (NPAIR[0] + 1))
                            pe.wait_ge(f_t[0], NG * (NPAIR[0] + 1))
                            pe.wait_ge(f_h[0], NG * NPAIR[0])
                        pe.wait_ge(xg_ready, NG * 2 + g + 1)
                    if step == "q":
                        ring_wait(j)
                        pe.matmul(bank[j % RING][:, :], w2[:, 0, c * P:(c + 1) * P], x,
                                  start=True, stop=True).then_inc(c_filled, 1)
                    elif step == "kv":
                        for m in range(4):
                            ring_wait(j + m)
                            pe.matmul(bank[(j + m) % RING][:, :], x[:, c * CH:(c + 1) * CH],
                                      w2[:, 1 + m // 2, (m % 2) * 512:(m % 2 + 1) * 512],
                                      start=True, stop=True).then_inc(c_filled, 1)
                    elif step == "kT":
                        for m in range(2):
                            ring_wait(j + m)
                            pe.wait_ge(c_comb, g * 16 + 8 + 2 * c + m + 1)
                            for t in range(4):
                                last = pe.transpose(bank[(j + m) % RING][:, t * P:(t + 1) * P],
                                                    k2[:, c % 2, (4 * m + t) * P:(4 * m + t + 1) * P], ident)
                            last.then_inc(c_filled, 1)
                    elif step == "sc":
                        pe.wait_ge(c_qb, n + 1)
                        for m in range(4):
                            ring_wait(j + m)
                            pe.wait_ge(c_kT, g * 8 + 2 * c + m // 2 + 1)
                            for t in range(2):
                                last = pe.matmul(bank[(j + m) % RING][:, t * 2 * CH:(t + 1) * 2 * CH],
                                                 kT2[:, 2 * m + t, :], qb2[:, c % 2, 2 * m + t, :, :],
                                                 start=True, stop=True)
                            last.then_inc(c_filled, 1)
                    elif step == "num":
                        wait(pe, c_y, n)
                        if c == 0:
                            pe.wait_ge(t_r, NG * 2 + g)
                        wait(pe, c_add, 3 * n)
                        pe.wait_ge(c_v, g * 8 + 2 * c + 2)
                        pe.wait_ge(c_mask, n * 4 + 4)
                        W = D2 + 1
                        for b, (p0, p1) in enumerate(UPAIRS):
                            for p in range(p0, p1):
                                o_ = (p - p0) * 2 * W
                                pe.matmul(bank[4 + b][:, o_:o_ + 2 * W], q2[:, p, c * CH:(c + 1) * CH],
                                          S2[:, p, :], start=True, stop=False)
                                for h in range(2):
                                    last = pe.matmul(bank[4 + b][:, o_ + h * W:o_ + (h + 1) * W],
                                                     probs[:, c % 2, 2 * p + h, :], v2[:, c % 2, 2 * p + h, :],
                                                     start=False, stop=(h == 1))
                        last.then_inc(c_num, 1)
                    elif step == "U":
                        for m, (p0, p1) in enumerate(UPAIRS):
                            ring_wait(j + m)
                            for p in range(p0, p1):
                                o_ = (p - p0) * 2 * (D2 + 1)
                                last = pe.matmul(bank[(j + m) % RING][:, o_:o_ + 2 * (D2 + 1)],
                                                 k2[:, c % 2, p * P:(p + 1) * P], v2[:, c % 2, 2 * p:2 * p + 2, :],
                                                 start=True, stop=True)
                            last.then_inc(c_filled, 1)
                    elif step == "yT":
                        pe.wait_ge(c_y, n + 1)
                        for m in range(2):
                            ring_wait(j + m)
                            for t in range(4):
                                q_ = 4 * m + t
                                last = pe.transpose(bank[(j + m) % RING][:, t * P:(t + 1) * P],
                                                    y2[:, 2 * q_:2 * q_ + 2, :], ident)
                            last.then_inc(c_filled, 1)
                    else:
                        pe.wait_ge(c_yT, g * 8 + 8)
                        for p in range(PAIRS):
                            last = pe.matmul(bank[4][:, :], w2o[:, p, :], yT2[:, p, :],
                                             start=(p == 0), stop=(p == PAIRS - 1))
                        last.then_inc(c_y_out, 1)

            def main(stage, g, par, hook):
                if stage == 0:
                    main0(g, par, hook)
                elif stage == 2:
                    main2(g, par, hook)
                else:
                    main13(stage // 2, g, par, hook)

            def tail(stage, g, par, k):
                n, rn = tails(stage, g), routes(stage, g)
                if stage == 0:
                    if k == 1:
                        wait(pe, t_cw, g)
                        pe.wait_ge(a_o, g + 1)
                        pe.matmul(T[:, :], mean_w, o[:, :], start=True, stop=True).then_inc(a_mean, 1)
                    elif k == 4:
                        pe.wait_ge(a_sq, g + 1)
                        pe.matmul(T[:, :], mean_w, sq[:, :], start=True, stop=True).then_inc(a_var, 1)
                    elif k == 8:
                        pe.wait_ge(a_og, g + 1)
                        pe.matmul(T[:, :], w0[:, 5, :], og[:, :], start=True, stop=True).then_inc(a_y, 1)
                    k -= ATTN_NORM_STEPS
                if k == 1:
                    pe.wait_ge(t_r, n + 1)
                    if stage == 1:
                        pe.wait_ge(t_cw, NG)
                    elif stage == 2:
                        wait(pe, t_cw, NG + g)
                    elif stage == 3:
                        pe.wait_ge(t_cw, 2 * NG)
                    wait(pe, t_std, n)
                    pe.matmul(T[:, :], mean_w, r[:, :], start=True, stop=True).then_inc(t_mean, 1)
                elif k == 4:
                    pe.wait_ge(t_sq, n + 1)
                    pe.matmul(T[:, :], mean_w, sq[:, :], start=True, stop=True).then_inc(t_var, 1)
                elif k == NORM_STEPS:
                    i = stage // 2
                    pe.wait_ge(t_xo, n + 1)
                    for c in range(NC):
                        last = pe.matmul(T[:, c * EXPERTS[i]:(c + 1) * EXPERTS[i]], xo[:, c * CH:(c + 1) * CH],
                                         w_route[i][:, :], start=True, stop=True)
                    last.then_inc(t_logit, 1)
                elif k == NORM_STEPS + 3:
                    pe.wait_ge(t_cwp, rn + 1)
                    for c in range(NC):
                        last = pe.transpose(T16[0:96, c * CH:(c + 1) * CH],
                                            parts[:, c, :, :], ident16[:, :])
                    last.then_inc(t_cwt, 1)

            pe.wait_ge(d_cst, 16)
            schedule(pe, main, tail)

        @block.scalar
        def _(act):
            def main0(g, par, hook):
                for i, step in enumerate(ORDER0):
                    hook(i)
                    if step == "q":
                        pe_count, b, slot = 1, 0, 0
                        wait(act, a_kv, g * 2 - 1)
                    elif step == "k":
                        pe_count, b, slot = 2, 1, 1
                        wait(act, a_kv, g * 2)
                    elif step == "kv01":
                        pe_count, b, slot = 4, 3, 0
                        act.wait_ge(a_q, g + 1)
                    elif step == "kv23":
                        pe_count, b, slot = 6, 0, 1
                        act.wait_ge(a_k, g + 1)
                    elif step == "g1":
                        act.wait_ge(a_proj, g * 6 + 3)
                        act.activation(g1[:, :], bank[2][:, :], ACT.Copy).then_inc(a_g1, 1)
                        continue
                    elif step == "gate":
                        act.wait_ge(a_proj, g * 6 + 5)
                        if not (isinstance(g, int) and g < 2):
                            act.wait_ge(a_og, g - 1)
                        act.activation(gate[:, par, :], bank[2][:, :], ACT.Sigmoid).then_inc(a_gate, 1)
                        continue
                    else:
                        continue
                    act.wait_ge(a_proj, g * 6 + pe_count)
                    act.activation(sig[:, slot, :], bank[b][:, :], ACT.Sigmoid).then_inc(a_sig, 1)

            def main13(i, g, par, hook):
                n = NPAIR[i] + 1
                for s in range(n):
                    hook(s)
                    act.wait_ge(f_g[i], g * n + s + 1)
                    wait(act, f_t[i], g * n + last_use(s, n, 2) + 1)
                    act.activation(fs[:, s % 2, :], bank[s % 2][:, :], ACT.Silu).then_inc(f_s[i], 1)

            def main2(g, par, hook):
                def relu_exp(j, m):
                    act.wait_ge(c_filled, g * JOBS + j + 1)
                    wait(act, c_comb, g * 16 + m - 1)
                    b = bank[j % RING]
                    act.activation(relu2[:, m % 2, :], b[:, :], ACT.Relu)
                    act.activation(exp2[:, m % 2, :], b[:, :], ACT.Exp).then_inc(c_er, 1)

                for i, (step, c) in enumerate(ORDER2):
                    hook(i)
                    j = FIRST[(step, c)]
                    if step == "q":
                        relu_exp(j, c)
                    elif step == "kv":
                        for m in range(2):
                            relu_exp(j + m, 8 + 2 * c + m)
                        for m in range(2):
                            act.wait_ge(c_filled, g * JOBS + j + 3 + m)
                            act.activation(v2[:, c % 2, 8 * m:8 * m + 8, 0:D2],
                                           bank[(j + 2 + m) % RING][:, :].rearrange("p (h d) -> p h d", d=D2),
                                           ACT.Copy).then_inc(c_v, 1)
                    elif step == "yT":
                        for m in range(2):
                            act.wait_ge(c_filled, g * JOBS + j + m + 1)
                            act.activation(yT2[:, 4 * m:4 * m + 4, c * CH:(c + 1) * CH],
                                           bank[(j + m) % RING][:, :].rearrange("p (q t) -> p q t", q=4),
                                           ACT.Copy).then_inc(c_yT, 1)

            def main(stage, g, par, hook):
                if stage == 0:
                    main0(g, par, hook)
                elif stage == 2:
                    main2(g, par, hook)
                else:
                    main13(stage // 2, g, par, hook)

            def tail(stage, g, par, k):
                n, rn = tails(stage, g), routes(stage, g)
                if stage == 0:
                    if k == 3:
                        act.wait_ge(a_c, g + 1)
                        act.activation(sq[:, :], c_[:, :], ACT.Square).then_inc(a_sq, 1)
                    elif k == 5:
                        act.wait_ge(a_var, g + 1)
                        act.activation(std[:, :], T[:, :], ACT.Sqrt, bias=eps).then_inc(a_std, 1)
                    k -= ATTN_NORM_STEPS
                if k == 3:
                    act.wait_ge(t_c, n + 1)
                    act.activation(sq[:, :], c_[:, :], ACT.Square).then_inc(t_sq, 1)
                elif k == 5:
                    act.wait_ge(t_var, n + 1)
                    act.activation(std[:, :], T[:, :], ACT.Sqrt, bias=eps).then_inc(t_std, 1)
                elif k == NORM_STEPS + 1:
                    i = stage // 2
                    act.wait_ge(t_logit, rn + 1)
                    wait(act, t_cwp, rn)
                    act.activation(sg[i][:, :, :, 0:EXPERTS[i] // RG],
                                   T[:, 0:NC * EXPERTS[i]].rearrange("p (c g k) -> p c g k", c=NC, g=RG),
                                   ACT.Sigmoid).then_inc(t_sig, 1)
                elif k == NORM_STEPS + 4:
                    i = stage // 2
                    act.wait_ge(t_cwt, rn + 1)
                    act.activation(CW[:, cols(g)], T16[0:96, 0:GROUP], ACT.Copy).then_inc(t_cw, 1)

            act.wait_ge(d_cst, 16)
            schedule(act, main, tail)

        @block.vector
        def _(dve):
            def main0(g, par, hook):
                for i, step in enumerate(ORDER0):
                    hook(i)
                    if step == "q":
                        dve.wait_ge(a_sig, g * 4 + 1)
                        wait(dve, a_attn, g * NC)
                        wait(dve, a_qs, g)
                        wait(dve, a_qbd, g)
                        dve.tensor_tensor(qT[:, :, :].rearrange("p c t -> p (c t)"), bank[0][:, :], sig[:, 0, :],
                                          ALU.mult).then_inc(a_q, 1)
                    elif step == "k":
                        dve.wait_ge(a_sig, g * 4 + 2)
                        for s in range(4):
                            p0, p1 = 32 * s, 32 * s + 32
                            last = dve.tensor_tensor(kz[p0:p1, s, :], bank[1][p0:p1, :], sig[p0:p1, 1, :], ALU.mult)
                        last.then_inc(a_k, 1)
                    elif step == "g1":
                        dve.wait_ge(a_q, g + 1)
                        for h in range(4):
                            last = dve.tensor_scalar(qbd[:, :, h, :], qT[:, :, :], cst[:, C_HEAD + h:C_HEAD + h + 1],
                                                     None, ALU.mult)
                        last.then_inc(a_qbd, 1)
                    elif step in ("kv01", "kv23"):
                        m = 0 if step == "kv01" else 1
                        dve.wait_ge(a_sig, g * 4 + 3 + m)
                        wait(dve, a_v, g * NC)
                        wait(dve, a_ks, g)
                        dve.tensor_tensor(KV[:, 2 * m:2 * m + 2, :, :].rearrange("p c k e -> p (c k e)"),
                                          bank[3 if m == 0 else 0][:, :], sig[:, m, :], ALU.mult).then_inc(a_kv, 1)
                    elif step[0] == "sc":
                        c = step[1]
                        n = g * NC + c
                        wait(dve, a_attn, n - 1)
                        for s in range(4):
                            dve.wait_ge(a_score, n * 4 + s + 1)
                            dve.tensor_tensor(probs[:, c % 2, 4 * s:4 * s + 4, :],
                                              bank[s][:, :].rearrange("p (h t) -> p h t", h=4),
                                              mask0[:, 4 * s:4 * s + 4, :], ALU.mult).then_inc(a_mask, 1)
                    elif step[0] == "pv":
                        c = step[1]
                        n = g * NC + c
                        dve.wait_ge(a_upd, n + 1)
                        wait(dve, a_state, n)
                        dve.tensor_tensor(upd[:, :], bank[5][:, 0:E], block0, ALU.mult).then_inc(a_updr, 1)
                        dve.wait_ge(a_updr, n + 1)
                        dve.wait_ge(a_attn, n + 1)
                        if par == 1 and c == NC - 1:
                            dve.memset(S0[:, :], 0.0).then_inc(a_state, 1)
                        else:
                            dve.scalar_tensor_tensor(out=S0[:, :], in0=S0[:, :], scalar=lamc, in1=upd[:, :],
                                                     op0=ALU.mult, op1=ALU.add).then_inc(a_state, 1)

            def main13(i, g, par, hook):
                n_pairs = NPAIR[i]
                n = n_pairs + 1

                def weigh(s):
                    dve.wait_ge(f_w[i], g * n_pairs + s + 1)
                    dve.wait_ge(f_t[i], g * n + s + 1)
                    wait(dve, f_d[i], g * n + last_use(s, n, 3) + 1)
                    dve.tensor_tensor(fh[:, s % 3, :], ft[:, s % 2, :], bank[4 + s % 2][:, :],
                                      ALU.mult).then_inc(f_h[i], 1)

                for s in range(n):
                    hook(s)
                    dve.wait_ge(f_s[i], g * n + s + 1)
                    dve.wait_ge(f_u[i], g * n + s + 1)
                    dst = ft[:, s % 2, :]
                    wait(dve, f_h[i], g * n_pairs + (s - 1 if s >= 2 else 0))
                    if s == n_pairs:
                        dst = fh[:, s % 3, :]
                        wait(dve, f_d[i], g * n + last_use(s, n, 3) + 1)
                    dve.tensor_tensor(dst, fs[:, s % 2, :], bank[2 + s % 2][:, :], ALU.mult).then_inc(f_t[i], 1)
                    if s >= 1:
                        weigh(s - 1)

            def main2(g, par, hook):
                W = D2 + 1

                def combine(dst, m):
                    dve.wait_ge(c_er, g * 16 + m + 1)
                    dve.scalar_tensor_tensor(out=dst, in0=exp2[:, m % 2, :], scalar=1.0, in1=relu2[:, m % 2, :],
                                             op0=ALU.min, op1=ALU.add).then_inc(c_comb, 1)

                for i, (step, c) in enumerate(ORDER2):
                    hook(i)
                    j = FIRST[(step, c)]
                    n = g * NC + c
                    if step == "q":
                        if c == 0:
                            wait(dve, c_num, g * NC)
                            wait(dve, c_qb, g * NC)
                        combine(q2[:, c, :], c)
                    elif step == "kv":
                        for m in range(2):
                            combine(k2[:, c % 2, m * 512:(m + 1) * 512], 8 + 2 * c + m)
                    elif step == "kT":
                        for m in range(2):
                            dve.wait_ge(c_filled, g * JOBS + j + m + 1)
                            dve.tensor_copy(kT2[:, 4 * m:4 * m + 4, :],
                                            bank[(j + m) % RING][:, :].rearrange("p (q t) -> p q t", q=4))\
                               .then_inc(c_kT, 1)
                    elif step == "sc":
                        wait(dve, c_num, n - 1)
                        for m in range(4):
                            dve.wait_ge(c_filled, g * JOBS + j + m + 1)
                            dve.tensor_tensor(probs[:, c % 2, 4 * m:4 * m + 4, :],
                                              bank[(j + m) % RING][:, :].rearrange("p (h t) -> p h t", h=4),
                                              tri[:, None, :].to_broadcast([P, 4, CH]), ALU.mult).then_inc(c_mask, 1)
                    elif step == "num":
                        dve.wait_ge(c_num, n + 1)
                        for b, (p0, p1) in enumerate(UPAIRS):
                            v = bank[4 + b][:, 0:(p1 - p0) * 2 * W].rearrange("p (h w) -> p h w", w=W)
                            last = dve.tensor_scalar(den2[:, 0, 2 * p0:2 * p1], v[:, :, D2], 1e-6, None, ALU.add)
                        last.then_inc(c_den, 1)
                        dve.wait_ge(c_den, 2 * n + 1)
                        dve.reciprocal(den2[:, 1, :], den2[:, 0, :]).then_inc(c_den, 1)
                        dve.wait_ge(c_den, 2 * n + 2)
                        if c == 0:
                            wait(dve, c_filled, g * JOBS - JOBS + FIRST[("yT", NC - 1)] + 2)
                        else:
                            dve.wait_ge(c_filled, g * JOBS + FIRST[("yT", c - 1)] + 2)
                        for b, (p0, p1) in enumerate(UPAIRS):
                            v = bank[4 + b][:, 0:(p1 - p0) * 2 * W].rearrange("p (h w) -> p h w", w=W)
                            last = dve.tensor_tensor(y2[:, 2 * p0:2 * p1, :], v[:, :, 0:D2],
                                                     den2[:, 1, 2 * p0:2 * p1, None].to_broadcast([P, 2 * (p1 - p0), D2]),
                                                     ALU.mult)
                        last.then_inc(c_y, 1)
                    elif step == "U":
                        for m, (p0, p1) in enumerate(UPAIRS):
                            if par == 1 and c == NC - 1:
                                dve.wait_ge(c_filled, g * JOBS + j + m + 1)
                                dve.memset(S2[:, p0:p1, :], 0.0).then_inc(c_add, 1)
                                continue
                            dve.wait_ge(c_filled, g * JOBS + j + m + 1)
                            u = bank[(j + m) % RING][:, 0:(p1 - p0) * 2 * W].rearrange("p (q w) -> p q w", w=2 * W)
                            for h in range(2):
                                rows, w_ = slice(64 * h, 64 * h + 64), slice(h * W, (h + 1) * W)
                                last = dve.tensor_tensor(S2[rows, p0:p1, w_], S2[rows, p0:p1, w_], u[rows, :, w_],
                                                         ALU.add)
                            last.then_inc(c_add, 1)

            def main(stage, g, par, hook):
                if stage == 0:
                    main0(g, par, hook)
                elif stage == 2:
                    main2(g, par, hook)
                else:
                    main13(stage // 2, g, par, hook)

            def route(i, rn):
                at = [0]
                before = (rn - NG * i) * ROUTE_OPS[i] + NG * i * ROUTE_OPS[0]

                def then(ins):
                    at[0] += 1
                    ins.then_inc(route_step, 1)
                    wait_apart(dve, route_step, before + at[0], passed_dve)

                sgi = sg[i][:, :, :, :].rearrange("p c g k -> p c (g k)")
                ch_t = ch[:, :, :].rearrange("p (c g) k -> p c (g k)", c=NC)
                then(dve.tensor_tensor(ch_t, sgi, rbias[i][:, None, :].to_broadcast([P, NC, RW]), ALU.add))
                for n in range(NC * RG):
                    last = dve.max(top8[:, n, :], ch[:, n, :])
                then(last)
                gsf = gs[:, :, :].rearrange("p c g -> p (c g)")
                then(dve.tensor_tensor(gsf, top8[:, :, 0], top8[:, :, 1], ALU.add))
                shape = [P, NC, RG, RG]
                other, own = gs[:, :, None, :].to_broadcast(shape), gs[:, :, :, None].to_broadcast(shape)
                then(dve.tensor_tensor(ge[:, :, :, :], other, own, ALU.is_ge))
                then(dve.tensor_tensor(gt[:, :, :, :], other, own, ALU.is_gt))
                then(dve.tensor_tensor(ge[:, :, :, :], ge[:, :, :, :], lower[:, None, :, :].to_broadcast(shape), ALU.mult))
                then(dve.tensor_tensor(gt[:, :, :, :], gt[:, :, :, :], upper[:, None, :, :].to_broadcast(shape), ALU.mult))
                then(dve.tensor_tensor(ge[:, :, :, :], ge[:, :, :, :], gt[:, :, :, :], ALU.add))
                then(dve.tensor_reduce(rank[:, :], ge[:, :, :, :].rearrange("p c i j -> p (c i) j"), AX.X, ALU.add))
                then(dve.tensor_scalar(rank[:, :], rank[:, :], 1.5, None, ALU.is_lt))
                if i == 1:
                    then(dve.tensor_scalar(fill[:, :], rank[:, :], -1.0, OUT_OF_GROUP, ALU.add, ALU.mult))
                kept = rank[:, :, None].to_broadcast([P, NC * RG, 8])
                then(dve.tensor_tensor(ch[:, :, :], ch[:, :, :], kept, ALU.mult))
                if i == 1:
                    then(dve.tensor_tensor(ch[:, :, :], ch[:, :, :], fill[:, :, None].to_broadcast([P, NC * RG, 8]), ALU.add))
                for c in range(NC):
                    last = dve.max(top[:, c, :], ch_t[:, c, :])
                then(last)
                if i == 1:
                    then(dve.memset(top[:, :, 4:8], PAD))
                for c in range(NC):
                    last = dve.match_replace(mr[:, c, :], top[:, c, :], ch_t[:, c, :], TAKEN)
                then(last)
                then(dve.tensor_tensor(mr[:, :, :], mr[:, :, :], ch_t, ALU.not_equal))
                then(dve.tensor_tensor(cw[:, :, :], mr[:, :, :], sgi, ALU.mult))
                then(dve.tensor_reduce(wsum[:, :], cw[:, :, :], AX.X, ALU.add))
                then(dve.tensor_scalar(wsum[:, :], wsum[:, :], 1e-20, None, ALU.add))
                then(dve.reciprocal(wsum[:, :], wsum[:, :]))
                then(dve.scalar_tensor_tensor(out=cw[:, :, :], in0=cw[:, :, :], scalar=SCALE,
                                              in1=wsum[:, :, None].to_broadcast([P, NC, RW]),
                                              op0=ALU.mult, op1=ALU.mult))
                then(dve.tensor_copy(parts[:, :, 0, :], cw[:, :, :]))
                then(dve.tensor_tensor(cw[:, :, :], cw[:, :, :], parts[:, :, 0, :], ALU.subtract))
                then(dve.tensor_copy(parts[:, :, 1, :], cw[:, :, :]))
                then(dve.tensor_tensor(mr[:, :, :], cw[:, :, :], parts[:, :, 1, :], ALU.subtract))
                assert at[0] == ROUTE_OPS[i]

            def tail(stage, g, par, k):
                n, rn = tails(stage, g), routes(stage, g)
                if stage == 0:
                    if k == 0:
                        dve.wait_ge(a_attn, g * NC + NC)
                        wait(dve, a_mean, g)
                        dve.tensor_copy(o[:, :], bank[4][:, :]).then_inc(a_o, 1)
                    elif k == 2:
                        dve.wait_ge(a_mean, g + 1)
                        dve.wait_ge(a_o, g + 1)
                        wait(dve, t_xo, n)
                        dve.tensor_tensor(c_[:, :], o[:, :], T[:, :], ALU.subtract).then_inc(a_c, 1)
                    elif k == 6:
                        dve.wait_ge(a_std, g + 1)
                        dve.reciprocal(rs[:, :], std[:, :]).then_inc(a_rs, 1)
                        dve.wait_ge(a_rs, g + 1)
                        dve.tensor_tensor(og[:, :], c_[:, :], rs[:, :], ALU.mult).then_inc(a_n, 1)
                    elif k == 7:
                        dve.wait_ge(a_n, g + 1)
                        dve.tensor_scalar(rs[:, :], og[:, :], gb[:, 0:1], gb[:, 1:2], ALU.mult, ALU.add).then_inc(a_gb, 1)
                        dve.wait_ge(a_gb, g + 1)
                        dve.wait_ge(a_gate, g + 1)
                        dve.tensor_tensor(og[:, :], rs[:, :], gate[:, par, :], ALU.mult).then_inc(a_og, 1)
                    k -= ATTN_NORM_STEPS
                if k == 0:
                    if stage == 0:
                        dve.wait_ge(a_y, g + 1)
                        dve.wait_ge(xg_ready, g + 1)
                    elif stage == 2:
                        dve.wait_ge(c_y_out, g + 1)
                    else:
                        i = stage // 2
                        dve.wait_ge(f_d[i], (g + 1) * (NPAIR[i] + 1))
                    if stage:
                        dve.wait_ge(xt_ready, NG * (stage - 1) + g + 1)
                    wait(dve, t_xo, n)
                    y = {0: T, 1: bank[6], 2: bank[4], 3: bank[6]}[stage]
                    dve.scalar_tensor_tensor(out=r[:, :], in0=XT[:, cols(g)], scalar=2.0 if stage == 3 else 1.0,
                                             in1=y[:, :], op0=ALU.mult, op1=ALU.add).then_inc(t_r, 1)
                elif k == 2:
                    dve.wait_ge(t_mean, n + 1)
                    dve.wait_ge(t_r, n + 1)
                    dve.tensor_tensor(c_[:, :], r[:, :], T[:, :], ALU.subtract).then_inc(t_c, 1)
                elif k == 6:
                    dve.wait_ge(t_std, n + 1)
                    dve.reciprocal(rs[:, :], std[:, :]).then_inc(t_rs, 1)
                    dve.wait_ge(t_rs, n + 1)
                    wait(dve, xt_ready, n)
                    dve.tensor_tensor(xo[:, :], c_[:, :], rs[:, :], ALU.mult).then_inc(t_xo, 1)
                elif k == NORM_STEPS + 2:
                    i = stage // 2
                    dve.wait_ge(t_sig, rn + 1)
                    wait(dve, t_cwt, rn)
                    wait(dve, t_cwp, rn)
                    route(i, rn)
                    dve.tensor_copy(parts[:, :, 2, :], mr[:, :, :]).then_inc(t_cwp, 1)

            dve.memset(vpad, 0.0).then_inc(init_v, 1)
            dve.memset(S0[:, :], 0.0).then_inc(init_v, 1)
            dve.memset(kz, 0.0).then_inc(init_v, 1)
            dve.wait_ge(d_cst, 16)
            dve.wait_ge(d_sel, 16)
            dve.tensor_copy(ident16[:, :], ident).then_inc(init_dve, 1)
            sel_stage = probs[0:96, :, :, :].rearrange("p a b c -> p (a b c)")
            for i, c0 in ((0, 0), (1, NPAIR[0] * P)):
                dve.tensor_copy(sel[i][:, :, :].rearrange("p s m -> p (s m)"),
                                sel_stage[:, c0:c0 + NPAIR[i] * P]).then_inc(init_dve, 1)
            dve.wait_ge(init_v, 3)
            dve.wait_ge(init_dve, 3)
            dve.wait_ge(d_w0, 16 * 10)
            schedule(dve, main, tail)

        @block.gpsimd
        def _(pool):
            def copy_x(stage, g, par):
                n = NG * stage + g
                if stage == 0:
                    if isinstance(g, int) and g == 0:
                        wait_apart(pool, d_x0, 16, passed_pool)
                    else:
                        wait_apart(pool, d_x, 16, passed_pool)
                else:
                    wait_apart(pool, xt_ready, n - NG + 1, passed_pool)
                old = isinstance(g, int) and g < 2
                gg = g + NG - 2 if old else g - 2
                user = stage - 1 if old else stage
                if user == 0:
                    wait_apart(pool, a_proj, gg * 6 + 6, passed_pool)
                elif user == 1 or user == 3:
                    wait_apart(pool, f_u[user // 2], gg * (NPAIR[user // 2] + 1) + NPAIR[user // 2] + 1, passed_pool)
                elif user == 2:
                    wait_apart(pool, c_filled, gg * JOBS + FIRST[("kv", NC - 1)] + 4, passed_pool)
                pool.tensor_copy(xg[:, par, :], XT[:, cols(g)]).then_inc(xg_ready, 1)

            def main0(g, par, hook):
                for i, step in enumerate(ORDER0):
                    hook(i)
                    if step == "q":
                        copy_x(0, g, par)
                    elif step == "k":
                        wait_apart(pool, a_q, g + 1, passed_pool)
                        pool.tensor_tensor(qs[:, :, :], qT[:, :, :], lamq[:, None, :].to_broadcast([P, NC, CH]),
                                           ALU.mult).then_inc(a_qs, 1)
                    elif step == "kv23":
                        wait_apart(pool, a_kv, g * 2 + 2, passed_pool)
                        pool.tensor_tensor(ks[:, :, :], KV[:, :, 0, :], lamk[:, None, :].to_broadcast([P, NC, E]),
                                           ALU.mult).then_inc(a_ks, 1)
                    elif step[0] == "sc":
                        c = step[1]
                        n = g * NC + c
                        wait_apart(pool, a_attn, n - 1, passed_pool)
                        dst = vpad[:, c % 2, :, :].rearrange("p h e -> p (h e)")
                        step_ = E + D0
                        for h in range(H0):
                            last = pool.tensor_copy(dst[:, h * step_:h * step_ + D0], KV[:, c, 1, h * D0:(h + 1) * D0])
                        last.then_inc(a_v, 1)

            def main13(stage, g, par, hook):
                for s in range(MAIN_HOOKS[stage]):
                    if s == 0:
                        hook(s)
                        copy_x(stage, g, par)
                    else:
                        hook(s)

            def main2(g, par, hook):
                for i, (step, c) in enumerate(ORDER2):
                    hook(i)
                    if i == 0:
                        copy_x(2, g, par)
                    if step == "kT":
                        n = g * NC + c
                        wait_apart(pool, c_comb, g * 16 + 8, passed_pool)
                        if c < 2:
                            wait_apart(pool, c_filled, g * JOBS - JOBS + FIRST[("sc", c + 2)] + 4, passed_pool)
                        else:
                            wait_apart(pool, c_filled, g * JOBS + FIRST[("sc", c - 2)] + 4, passed_pool)
                        for h in range(2):
                            last = pool.tensor_scalar(qb2[:, c % 2, :, h, :], q2[:, :, c * CH:(c + 1) * CH],
                                                      cst[:, C_HALF + h:C_HALF + h + 1], 0.0, ALU.mult, ALU.add)
                        last.then_inc(c_qb, 1)

            def main(stage, g, par, hook):
                if stage == 0:
                    main0(g, par, hook)
                elif stage == 2:
                    main2(g, par, hook)
                else:
                    main13(stage, g, par, hook)

            def tail(stage, g, par, k):
                if stage == 0:
                    k -= ATTN_NORM_STEPS
                if k == 7:
                    n = tails(stage, g)
                    wait_apart(pool, t_xo, n + 1, passed_pool)
                    pool.tensor_copy(XT[:, cols(g)], xo[:, :]).then_inc(xt_ready, 1)

            pool.memset(w0[:, 3:5, :], 0.0).then_inc(init_pool, 1)
            pool.memset(rbias[1][:, :], PAD).then_inc(init_pool, 1)
            pool.memset(sg[1][:, :, :, :], 0.0).then_inc(init_s2, 1)
            pool.memset(v2[:, :, :, :], 1.0).then_inc(init_s2, 1)
            pool.memset(S2[:, :, :], 0.0).then_inc(init_s2, 1)
            schedule(pool, main, tail)


def constants():
    start = 2.0 ** (-2.0 ** (-(np.log2(H0) - 3)))
    slopes = np.array([start * start ** i for i in range(H0)], np.float32) * np.float32(1.0 + 1e-05)
    s = slopes.astype(np.float64)
    t = np.arange(CH)
    diff = t[None, :] - t[:, None]
    c = np.zeros((P, C_END), np.float32)
    mask = np.where(diff[:, None, :] >= 0, np.exp(-s[None, :, None] * np.maximum(diff, 0)[:, None, :]), 0.0)
    c[:, C_MASK0:C_LAMQ] = mask.reshape(P, -1)
    head = np.arange(E) // D0
    c[:, C_LAMQ:C_LAMK] = np.exp(-s[head][:, None] * (t[None, :] + 1.0))
    c[:, C_LAMK:C_BLOCK] = np.exp(-s[head][None, :] * (CH - 1.0 - t[:, None]))
    c[:, C_BLOCK:C_TRI] = head[:, None] == head[None, :]
    c[:, C_TRI:C_IDENT] = diff >= 0
    c[:, C_IDENT:C_MEAN] = np.eye(P)
    c[:, C_MEAN:C_HEAD] = 1.0 / E
    c[:, C_HEAD:C_LOWER] = (head % 4)[:, None] == np.arange(4)[None, :]
    i, j = np.arange(RG)[:, None], np.arange(RG)[None, :]
    c[:, C_LOWER:C_UPPER] = (j < i).reshape(-1)
    c[:, C_UPPER:C_LAMC] = (j > i).reshape(-1)
    c[:, C_LAMC] = np.exp(-s[head] * CH)
    c[:, C_EPS] = 1e-5
    c[:, C_HALF:C_END] = (np.arange(P) // D2)[:, None] == np.arange(2)[None, :]
    rows = np.zeros((3, RW, NPAIR[0] + NPAIR[1], P), np.float32)
    at = 0
    for n in EXPERTS:
        for e in range(n):
            col = (e // (n // RG)) * 8 + e % (n // RG)
            rows[:, col, at + e // 2, (e % 2) * INNER:(e % 2 + 1) * INNER] = 1.0
        at += n // 2
    return c, rows.reshape(96, -1)


def arrange(inputs):
    z = {k: np.asarray(v) for k, v in inputs.items()}
    cst, sel = constants()
    d = {"cst": cst, "sel": sel, "x": z["L0_attn_x"].reshape(TOK, E).T}
    for n in ("Wq", "Wk", "Wv", "Wo", "Wg1", "Wg2"):
        d["a" + n] = z["L0_attn_" + n]
    d["gamma"], d["beta"] = z["L0_attn_gamma"].reshape(E, 1), z["L0_attn_beta"].reshape(E, 1)
    experts = (("L0_ffn_expert_gate", "L0_ffn_expert_up", "L0_ffn_expert_down",
                "L0_ffn_shared_gate", "L0_ffn_shared_up", "L0_ffn_shared_down"),
               ("L1_ffn_Wg", "L1_ffn_Wu", "L1_ffn_Wd", "L1_ffn_Ws_g", "L1_ffn_Ws_u", "L1_ffn_Ws_d"))
    for i, (g, u, w, sg, su, sd) in enumerate(experts):
        n = NPAIR[i]
        gu = [np.concatenate([z[m].reshape(n, P, E), z[s].reshape(1, P, E)]) for m, s in ((g, sg), (u, su))]
        d[f"gu{i}"] = np.stack(gu, 1).transpose(3, 0, 1, 2)
        down = z[w].transpose(0, 2, 1).reshape(n, P, E)
        d[f"dn{i}"] = np.concatenate([down, z[sd].T.reshape(1, P, E)]).transpose(1, 0, 2)
    d["gw1"], d["gw3"] = z["L0_ffn_gate_w"].T, z["L1_ffn_gate_w"].T
    d["gb1"] = np.broadcast_to(z["L0_ffn_gate_bias"], (P, EXPERTS[0]))
    d["gb3"] = np.broadcast_to(z["L1_ffn_gate_bias"], (P, EXPERTS[1]))
    d["w2"] = np.stack([z["L1_attn_" + n] for n in ("Wq", "Wk", "Wv")], 1)
    d["w2o"] = z["L1_attn_Wo"].reshape(PAIRS, P, E).transpose(1, 0, 2)
    return {k: np.ascontiguousarray(v) for k, v in d.items()}


def kernel(**inputs):
    import concourse.bacc as bacc
    from concourse.bass_utils import run_bass_kernel_spmd

    nc = bacc.Bacc("TRN2", target_bir_lowering=False, num_devices=1)
    data = arrange(inputs)
    arrays = {f"in_{k}": v for k, v in data.items()}
    handles = {k: nc.dram_tensor(f"in_{k}", v.shape, mybir.dt.from_np(v.dtype), kind="ExternalInput").ap()
               for k, v in data.items()}
    out = nc.dram_tensor("out", (E, TOK), F32, kind="ExternalOutput").ap()
    build(nc, handles, out)
    got = run_bass_kernel_spmd(nc, [arrays], core_ids=[0]).results[0]["out"]
    return np.ascontiguousarray(got.T).reshape(BATCH, SEQ, E)
```

```python
from contextlib import ExitStack

import numpy as np

import concourse.bass as bass
from concourse import mybir

F32 = mybir.dt.float32
F32R = mybir.dt.float32r
BF16 = mybir.dt.bfloat16
ALU = mybir.AluOpType
ACT = mybir.ActivationFunctionType
AX = mybir.AxisListType

P = 128
E = 128
BATCH, SEQ = 4, 1024
TOK = BATCH * SEQ
GROUP = 512
NG = TOK // GROUP
CH = 128
NC = GROUP // CH
H0, D0 = 16, 8
H2, D2 = 16, 64
PAIRS = H2 // 2
EXPERTS = (32, 16)
INNER = 64
NPAIR = tuple(n // 2 for n in EXPERTS)
RW = 32
RG = 4
PAD = -2e30
OUT_OF_GROUP = 1e30
TAKEN = -3e38
SCALE = 2.5

C_MASK0 = 0
C_LAMQ = C_MASK0 + H0 * CH
C_LAMK = C_LAMQ + CH
C_BLOCK = C_LAMK + E
C_TRI = C_BLOCK + E
C_IDENT = C_TRI + CH
C_MEAN = C_IDENT + P
C_HEAD = C_MEAN + P
C_LOWER = C_HEAD + 4
C_UPPER = C_LOWER + RG * RG
C_LAMC = C_UPPER + RG * RG
C_HALF = C_LAMC + 1
C_QUARTER = C_HALF + 2
C_END = C_QUARTER + 4

UNITS0 = [(s, 0, 0) for s in ("q", "k", "g1", "kv01", "gate", "kv23")]
UNITS0 += [(s, c, m) for c in range(NC) for s in ("sc", "pv") for m in range(4)]


def units_ffn(i):
    return [(s, k, 0) for k in range(NPAIR[i] + 1) for s in ("gate", "up", "weight", "down")]


RING = 4
PARTS = {"q": 1, "kv": 4, "kT": 2, "sc": 4, "num": 3, "U": 3, "yT": 2}


def units2():
    order = [("q", p) for p in range(PAIRS)] + [("kv", 0), ("kv", 1), ("kT", 0)]
    for c in range(NC):
        order.append(("sc", c))
        order.append(("U", c))
        if c:
            order.append(("yT", c - 1))
        if c + 1 < NC:
            order.append(("kT", c + 1))
        order.append(("num", c))
        if c + 2 < NC:
            order.append(("kv", c + 2))
    order.append(("yT", NC - 1))
    return [(s, c, m) for s, c in order for m in range(PARTS[s])]


UNITS2 = units2()
RING_JOBS = [u for u in UNITS2 if u[0] != "num"]
JOB = {u: j for j, u in enumerate(RING_JOBS)}
JOBS = len(RING_JOBS)
assert JOBS % RING == 0
QB_AT = {("kv", 1, 3): 0, ("kT", 0, 1): 1, ("num", 0, 0): 2, ("num", 1, 0): 3}


def qb_free(g, c):
    return (g - 1) * JOBS + JOB[("sc", c + 2, 3)] + 1 if c < 2 else g * JOBS + JOB[("sc", c - 2, 3)] + 1


UNITS = (UNITS0, units_ffn(0), UNITS2, units_ffn(1))
UPAIRS = ((0, 3), (3, 6), (6, 8))

LAG = 3
TAIL = (
    (("o", 1), ("amean", 2), ("ac", 0), ("asq", 1.5), ("avar", 2.5), ("ave", 1), ("apow", 0.5), ("abc", 2),
     ("an", 0), ("agb", 1), ("aog", 0), ("awo", 2), ("r", 1), ("mean", 3), ("c", 1), ("sq", 0.5), ("var", 2.5),
     ("ve", 1), ("pow", 1.5), ("bc", 1), ("xo", 0), ("xt", 1), ("logit", 0.5), ("sig", 1), (0, 3), (1, 2.5),
     (2, 9), (3, 1), (4, 0.5), (5, 1), (6, 5), (7, 3), (8, 2), ("cwT", 6), ("cw", 1.5)),
    (("h1", 2), ("d0", 6), ("h2", 0), ("d1", 1), ("d2", 2), ("r", 3), ("mean", 0.5), ("c", 1), ("sq", 1),
     ("var", 2), ("ve", 0), ("pow", 1.5), ("bc", 5), ("xo", 0)),
    (("wo0", 1.5), ("wo1", 6), ("wo2", 2), ("wo3", 2.5), ("r", 0), ("mean", 2), ("c", 2), ("sq", 0),
     ("var", 3.5), ("ve", 1), ("pow", 0.5), ("bc", 2), ("xo", 1), ("xt", 0), ("logit", 2), ("sig", 0.5), (0, 1),
     (1, 11), (2, 1.5), (3, 2), (4, 3), (5, 2), (6, 3), (7, 2), (8, 5), ("cwT", 6), ("cw", 0)),
    (("h1", 0), ("d0", 2), ("h2", 2), ("d1", 1.5), ("d2", 2.5), ("r", 2), ("mean", 1), ("c", 5), ("sq", 3),
     ("var", 3.5), ("ve", 0.5), ("pow", 0), ("bc", 4), ("xo", 0)),
)
DRAIN = ("h1", "d0", "h2", "d1", "d2")
ROUTE_OPS = ((2, 3, 3, 1, 1, 1, 3, 3, 4), (4, 3, 3, 3, 2, 1, 3, 3, 4))


def emptied(job):
    step, c, m = job
    if step == "q":
        return "er", 16, c + 1
    if step == "kv":
        return ("er", 16, 8 + 2 * c + m + 1) if m < 2 else ("v", 8, 2 * c + m - 1)
    return {"kT": ("kT", 8, 2 * c + m + 1), "sc": ("mask", 16, 4 * c + m + 1),
            "U": ("u", 12, 3 * c + m + 1), "yT": ("yT", 8, 2 * c + m + 1)}[step]


def following(stage, g):
    return (stage + 1, 0) if isinstance(g, int) and g == NG - 1 else (stage, g + 1)


X_AT = tuple(UNITS[k].index(u) for k, u in enumerate((("sc", 2, 0), ("gate", NPAIR[0] - 2, 0), ("sc", 2, 0),
                                                       ("gate", NPAIR[1] - 2, 0))))


def placed(steps, n):
    at, total = 0.0, sum(d for _, d in steps)
    where = []
    for name, d in steps:
        at += d
        where.append((name, min(n - 1, int(at * min(1.0, (n - 1) / total)))))
    return where


def schedule(eng, main, tail):
    def hooked(stage, prev_stage, prev_g, prev_parity):
        steps = TAIL[prev_stage]
        if stage != prev_stage:
            steps = [(name, 0 if name in DRAIN else d) for name, d in steps]
        where = placed(steps, len(UNITS[stage]))

        def hook(u):
            for name, at in where:
                if at == u:
                    tail(prev_stage, prev_g, prev_parity, name)
        return hook

    for stage in range(4):
        if stage:
            main(stage, 0, 0, hooked(stage, stage - 1, NG - 1, 1))
        else:
            main(stage, 0, 0, lambda u: None)
        main(stage, 1, 1, hooked(stage, stage, 0, 0))
        with eng.Fori(0, (NG - 4) // 2) as b:
            main(stage, b * 2 + 2, 0, hooked(stage, stage, b * 2 + 1, 1))
            main(stage, b * 2 + 3, 1, hooked(stage, stage, b * 2 + 2, 0))
        main(stage, NG - 2, 0, hooked(stage, stage, NG - 3, 1))
        main(stage, NG - 1, 1, hooked(stage, stage, NG - 2, 0))
    for name, _ in TAIL[3]:
        tail(3, NG - 1, 1, name)


def last_use(s, n, m):
    return s - m if s >= m else max(t for t in range(n) if t % m == s % m) - n


def wait(eng, sem, value):
    if not isinstance(value, int) or value > 0:
        eng.wait_ge(sem, value)


def wait_apart(eng, sem, value, passed):
    if isinstance(value, int):
        wait(eng, sem, value)
    else:
        eng.wait_ge(sem, value)
        eng.sem_inc(passed, 1)


def build(nc, a, out):
    with ExitStack() as ctx:
        def sb(name, shape, dt=F32):
            return ctx.enter_context(nc.sbuf_tensor(name, shape, dt))

        def slab(name, columns):
            at = -(-nc.sbuf_base // 32) * 32
            tensor = sb(name, [P, columns])
            assert nc.sbuf_base == at + columns * 4
            return tensor, at

        def over(name, at, shape):
            return nc.alloc_sbuf_tensor_at(name, shape, F32R, offset=at)

        def sem(name):
            return ctx.enter_context(nc.semaphore(name))

        bank = [ctx.enter_context(nc.psum_tensor(f"bank{i}", [P, GROUP], F32)) for i in range(8)]
        T = bank[7]
        T16 = T[:].bitcast(BF16)
        cst = sb("cst", [P, C_END])
        XT = sb("XT", [P, TOK])
        x_flat, at_x = slab("x_group", 2 * GROUP)
        x_group = x_flat[:, :].rearrange("p (b t) -> p b t", b=2)
        x_hi = over("x_hi", at_x, [P, 2, GROUP])
        x_lo = sb("x_lo", [P, 2, GROUP], F32R)
        w0 = sb("w0", [P, 6, E])
        gb = sb("gb", [P, 2])
        w_ffn, at_ffn = slab("w_ffn", (NPAIR[0] + 1) * 3 * E)
        w_f = [w_ffn[:, 0:(n + 1) * 3 * E].rearrange("p (s k e) -> p s k e", k=3, e=E) for n in NPAIR]
        w_lo = [over(f"w_lo{i}", at_ffn, [P, NPAIR[i] + 1, 3, E]) for i in range(2)]
        w2_flat, at_w2 = slab("w2", 3 * H2 * D2)
        w2 = w2_flat[:, :].rearrange("p (k e) -> p k e", k=3)
        sel_stage = w2_flat[0:96, 0:(NPAIR[0] + NPAIR[1]) * P]
        w2_lo = over("w2_lo", at_w2, [P, 3, H2 * D2])
        w2_hi = over("w2_hi", at_ffn + (NPAIR[1] + 1) * 3 * E * 4, [P, 3, H2 * D2])
        w2o = sb("w2o", [P, PAIRS, E])
        w_route = [sb(f"w_route{i}", [P, EXPERTS[i]]) for i in range(2)]
        rbias = [sb(f"rbias{i}", [P, RW]) for i in range(2)]
        ident16 = sb("ident16", [P, P], BF16)
        sel = [sb(f"sel{i}", [96, NPAIR[i], P], BF16) for i in range(2)]
        CW = sb("CW", [96, TOK], BF16)
        probs = sb("probs", [P, 2, 16, CH])
        arena, at_arena = slab("arena", 3 * 4096 + 1024)
        arena1 = arena[:, 0:4096]
        arena2 = arena[:, 4096:8192]
        arena3 = arena[:, 8192:12288]
        arena4 = arena[:, 12288:13312]
        w_hi = [over(f"w_hi{i}", at_arena, [P, NPAIR[i] + 1, 3, E]) for i in range(2)]
        h_hi = over("h_hi", at_arena + 8192 * 4, [P, 3, GROUP])
        h_lo = over("h_lo", at_arena + (8192 + 3 * GROUP) * 4, [P, 3, GROUP])
        sig = arena3[:, 0:1024].rearrange("p (b t) -> p b t", b=2)
        qT = arena3[:, 1024:1536].rearrange("p (c t) -> p c t", c=NC)
        kz = arena1[:, 0:2048].rearrange("p (q t) -> p q t", q=4)
        qbd = arena1[:, 2048:4096].rearrange("p (c r t) -> p c r t", c=NC, r=4)
        vpad = arena2[:, :].rearrange("p (b h e) -> p b h e", b=2, h=H0)
        qs = arena3[:, 1536:2048].rearrange("p (c t) -> p c t", c=NC)
        ks = arena3[:, 2048:2560].rearrange("p (c t) -> p c t", c=NC)
        KV = arena3[:, 2560:3584].rearrange("p (c k t) -> p c k t", c=NC, k=2)
        g1 = arena3[:, 3584:4096]
        gate = sb("gate", [P, 2, GROUP])
        S0 = sb("S0", [P, E])
        upd = sb("upd", [P, E])
        o = arena4[:, 0:GROUP]
        og = arena4[:, GROUP:2 * GROUP]
        fs = sb("fs", [P, 2, GROUP])
        ft = sb("ft", [P, 2, GROUP])
        y_or_h = sb("y_or_h", [P, 2, GROUP])
        fh = [y_or_h[:, 0, :], y_or_h[:, 1, :], arena3[:, 3072:3584]]
        q2 = arena1[:, :].rearrange("p (r t) -> p r t", r=PAIRS)
        yT2 = arena2[:, :].rearrange("p (r t) -> p r t", r=PAIRS)
        relu2 = fs
        exp2 = ft
        k2 = cst[:, C_MASK0:C_LAMQ].rearrange("p (b t) -> p b t", b=2)
        v2 = sb("v2", [P, 2, H2, D2 + 1])
        kT2 = arena4[:, :].rearrange("p (r t) -> p r t", r=PAIRS)
        qb2 = arena3[:, :].rearrange("p (b r h t) -> p b r h t", b=2, r=PAIRS, h=2)
        S2 = sb("S2", [P, PAIRS, 2 * (D2 + 1)])
        den2 = sb("den2", [P, 2, H2])
        u2 = sb("u2", [P, PAIRS, 2 * (D2 + 1)])
        y2 = y_or_h[:, :, :].rearrange("p b (h d) -> p (b h) d", d=D2)
        r = sb("r", [P, GROUP])
        sq = sb("sq", [P, GROUP])
        ogb = sq
        var = sb("var", [P, NC])
        rstd = sb("rstd", [P, NC])
        minus_half = sb("minus_half", [P, NC])
        xo = sb("xo", [P, GROUP])
        sg = [sb(f"sg{i}", [P, NC, RG, 8]) for i in range(2)]
        ch = sb("ch", [P, NC * RG, 8])
        top8 = sb("top8", [P, NC * RG, 8])
        gs = sb("gs", [P, NC, RG])
        ge = sb("ge", [P, NC, RG, RG])
        gt = sb("gt", [P, NC, RG, RG])
        rank = sb("rank", [P, NC * RG])
        fill = sb("fill", [P, NC * RG])
        top = sb("top", [P, NC, 8])
        mr = sb("mr", [P, NC, RW])
        wsum = sb("wsum", [P, NC])
        cw = sb("cw", [P, NC, RW])
        parts = sb("parts", [P, NC, 3, RW], BF16)

        mask0 = cst[:, C_MASK0:C_LAMQ].rearrange("p (h t) -> p h t", h=H0)
        lamq = cst[:, C_LAMQ:C_LAMK]
        lamk = cst[:, C_LAMK:C_BLOCK]
        block0 = cst[:, C_BLOCK:C_TRI]
        tri = cst[:, C_TRI:C_IDENT]
        ident = cst[:, C_IDENT:C_MEAN]
        mean_w = cst[:, C_MEAN:C_HEAD]
        lower = cst[:, C_LOWER:C_UPPER].rearrange("p (i j) -> p i j", i=RG)
        upper = cst[:, C_UPPER:C_LAMC].rearrange("p (i j) -> p i j", i=RG)
        lamc = cst[:, C_LAMC:C_LAMC + 1]

        d_x0, d_x = sem("x_group0_loaded"), sem("x_loaded")
        d_mask, d_wg = sem("masks_loaded"), sem("gate_weights_loaded")
        d_tail = sem("norm_and_router_weights_loaded")
        d_cst, d_w0, d_sel = sem("constants_loaded"), sem("stage0_weights_loaded"), sem("selectors_loaded")
        d_w13 = [sem("stage1_weights_loaded"), sem("stage3_weights_loaded")]
        d_w2 = sem("stage2_weights_loaded")
        d_out = sem("output_stored")
        init_pool, ident_ready, sel_ready = sem("pool_init_done"), sem("ident16_ready"), sem("selectors_ready")
        passed_pool, passed_dve = sem("passed_pool"), sem("passed_dve")
        init_half = sem("minus_half_ready")
        init_v, init_s2 = sem("stage0_buffers_zeroed"), sem("stage2_buffers_set")
        x_ready = sem("x_group_ready")
        xh_ready, xl_ready = sem("x_hi_ready"), sem("x_lo_ready")
        f_wh = [sem(f"f{i}_weights_hi_ready") for i in (1, 3)]
        f_wl = [sem(f"f{i}_weights_lo_ready") for i in (1, 3)]
        f_hh = [sem(f"f{i}_hidden_hi_ready") for i in (1, 3)]
        f_hl = [sem(f"f{i}_hidden_lo_ready") for i in (1, 3)]
        c_wh, c_wl = sem("c_weights_hi_ready"), sem("c_weights_lo_ready")
        a_proj = sem("a_projection_ready")
        a_sig = sem("a_sigmoid_ready")
        a_g1 = sem("a_g1_ready")
        a_gate = sem("a_gate_ready")
        a_q, a_k, a_kv = sem("a_q_ready"), sem("a_k_ready"), sem("a_kv_ready")
        a_qbd, a_kz = sem("a_qbd_ready"), sem("a_k_quarter_ready")
        a_qs, a_ks, a_v = sem("a_qscaled_ready"), sem("a_kscaled_ready"), sem("a_vpad_ready")
        a_score, a_mask = sem("a_scores_ready"), sem("a_masked_ready")
        a_upd, a_updr, a_state = sem("a_update_ready"), sem("a_update_read"), sem("a_state_ready")
        a_attn = sem("a_attention_ready")
        a_o, a_mean, a_c, a_sq, a_var, a_ve = (
            sem("a_norm_" + n) for n in ("o", "mean", "centred", "square", "var", "var_eps"))
        a_rs, a_bc, a_n, a_gb, a_og = (sem("a_norm_" + n) for n in ("rstd", "rstd_rows", "out", "affine", "gated"))
        f_g, f_u, f_w = ([sem(f"f{i}_{n}_ready") for i in (1, 3)] for n in ("gate", "up", "weight"))
        f_s, f_t, f_h = ([sem(f"f{i}_{n}_ready") for i in (1, 3)] for n in ("silu", "su", "hidden"))
        f_d = [sem(f"f{i}_down_done") for i in (1, 3)]
        c_filled = sem("c_ring_filled")
        c_er = sem("c_relu_exp_ready")
        c_comb = sem("c_features_ready")
        c_v, c_yT = sem("c_v_ready"), sem("c_yT_ready")
        c_u = sem("c_update_read")
        c_kT, c_mask = sem("c_kT_ready"), sem("c_masked_ready")
        c_qb0, c_qb1 = sem("c_qbd_first_ready"), sem("c_qbd_second_ready")
        c_num, c_y, c_add = sem("c_numerator_ready"), sem("c_y_ready"), sem("c_state_added")
        c_empty = {"er": c_er, "v": c_v, "kT": c_kT, "mask": c_mask, "u": c_u, "yT": c_yT}
        c_den = sem("c_denominator_step")
        a_y, c_y_out = sem("a_output_ready"), sem("c_output_ready")
        t_r, t_mean, t_c, t_sq, t_var, t_ve, t_rs, t_bc, t_xo = (
            sem("t_" + n)
            for n in ("residual", "mean", "centred", "square", "var", "var_eps", "rstd", "rstd_rows", "xo"))
        xt_ready = sem("xt_ready")
        t_logit, t_sig, t_cwp, t_cwt, t_cw = (
            sem("t_" + n) for n in ("logits", "scores", "weight_parts", "weights_transposed", "weights"))
        route_step = sem("route_step")

        block = ctx.enter_context(nc.Block())

        def cols(g):
            return bass.ds(g * GROUP, GROUP)

        def tails(stage, g):
            return g + NG * stage

        def routes(stage, g):
            return g + NG * (stage // 2)

        def stored(stage, g):
            return (t_xo, tails(stage, g) + 1) if stage % 2 else (xt_ready, routes(stage, g) + 1)

        def w_piece(t, k):
            return t[:, k // 2, (k % 2) * 512:(k % 2 + 1) * 512]

        def w_pieces_at(u, step, c):
            return (0, 1) if u == 0 else (c + 1,) if step == "q" and 1 <= c <= 4 else ()

        @block.sync
        def _(sp):
            sp.dma_start(x_flat[:, 0:GROUP], a["x"][:, 0:GROUP]).then_inc(d_x0, 16)
            sp.dma_start(w0[:, 0:4, :], a["aW"]).then_inc(d_w0, 16)
            sp.wait_ge(init_pool, 2)
            sp.dma_start(w0[:, 4, 0:D0], a["aWg1"]).then_inc(d_wg, 16)
            sp.dma_start(w0[0:D0, 5, :], a["aWg2"]).then_inc(d_wg, 16)
            sp.dma_start(cst[:, C_LAMQ:C_END], a["cst"][:, C_LAMQ:C_END]).then_inc(d_cst, 16)
            sp.dma_start(cst[:, C_MASK0:C_LAMQ], a["cst"][:, C_MASK0:C_LAMQ]).then_inc(d_mask, 16)
            sp.dma_start(gb[:, :], a["gb"]).then_inc(d_tail, 16)
            sp.dma_start(w_route[0][:, :], a["gw1"]).then_inc(d_tail, 16)
            sp.dma_start(rbias[0][:, :], a["gb1"]).then_inc(d_tail, 16)
            sp.dma_start(XT[:, :], a["x"]).then_inc(d_x, 16)
            sp.dma_start(sel_stage, a["sel"]).then_inc(d_sel, 16)
            for i in range(2):
                if i == 1:
                    sp.wait_ge(f_d[0], NG * (NPAIR[0] + 1))
                sp.dma_start(w_f[i], a[f"w{i}"]).then_inc(d_w13[i], 16)
                if i == 0:
                    sp.wait_ge(sel_ready, 2)
                    sp.dma_start(w2[:, :, :], a["w2"]).then_inc(d_w2, 16)
                    sp.dma_start(w2o[:, :, :], a["w2o"]).then_inc(d_w2, 16)
                    sp.dma_start(w_route[1][:, :], a["gw3"]).then_inc(d_w2, 16)
                    sp.dma_start(rbias[1][:, :].rearrange("p (g k) -> p g k", g=RG)[:, :, 0:4],
                                 a["gb3"].rearrange("p (g k) -> p g k", g=RG)).then_inc(d_w2, 16)
            for g in range(NG):
                sp.wait_ge(*stored(3, g))
                sp.dma_start(out[:, g * GROUP:(g + 1) * GROUP], XT[:, g * GROUP:(g + 1) * GROUP]).then_inc(d_out, 16)
            sp.wait_ge(d_out, 16 * NG)

        @block.tensor
        def _(pe):
            def product(out_, w, w_rest, x, x_rest, start=True, stop=True):
                pe.matmul(out_, w, x, start=start, stop=False)
                pe.matmul(out_, w, x_rest, start=False, stop=False)
                return pe.matmul(out_, w_rest, x, start=False, stop=stop)

            def main0(g, par, hook):
                x = x_group[:, par, :]
                for u, (step, c, m) in enumerate(UNITS0):
                    hook(u)
                    n = g * NC + c
                    if step == "q":
                        if isinstance(g, int) and g == 0:
                            pe.wait_ge(d_w0, 16)
                            pe.wait_ge(d_x0, 16)
                        else:
                            pe.wait_ge(x_ready, g)
                        wait(pe, a_mask, g * 16)
                        pe.matmul(bank[0][:, :], w0[:, 0, :], x, start=True, stop=True).then_inc(a_proj, 1)
                    elif step == "k":
                        pe.matmul(bank[1][:, :], w0[:, 1, :], x, start=True, stop=True).then_inc(a_proj, 1)
                    elif step == "g1":
                        if isinstance(g, int) and g == 0:
                            pe.wait_ge(d_wg, 32)
                        pe.matmul(bank[2][:, :], w0[:, 4, :], x, start=True, stop=True).then_inc(a_proj, 1)
                    elif step in ("kv01", "kv23"):
                        b, c0 = (bank[3], 0) if step == "kv01" else (bank[0], 2)
                        if step == "kv23":
                            pe.wait_ge(a_q, g + 1)
                        for c in (c0, c0 + 1):
                            last = pe.matmul(b[:, (c - c0) * 2 * E:(c - c0 + 1) * 2 * E],
                                             x[:, c * CH:(c + 1) * CH], w0[:, 1:3, :], start=True, stop=True)
                        last.then_inc(a_proj, 1)
                    elif step == "gate":
                        pe.wait_ge(a_g1, g + 1)
                        pe.matmul(bank[2][:, :], w0[:, 5, :], g1[:, :], start=True, stop=True).then_inc(a_proj, 1)
                    elif step == "sc":
                        if c == 0 and m == 0:
                            pe.wait_ge(a_qbd, g + 1)
                            pe.wait_ge(a_kv, g * 2 + 2)
                            pe.wait_ge(a_gate, g + 1)
                        if c == 0:
                            pe.wait_ge(a_kz, g * 4 + m + 1)
                        if c:
                            pe.wait_ge(a_mask, n * 4 - 3 + m)
                        pe.matmul(bank[m][:, :], kz[:, m, c * CH:(c + 1) * CH],
                                  qbd[:, c, :, :], start=True, stop=True).then_inc(a_score, 1)
                    elif step == "pv":
                        oc = bank[4][:, c * CH:(c + 1) * CH]
                        if m == 0:
                            if isinstance(g, int) and n == 0:
                                pe.wait_ge(init_v, 2)
                            if c == 0:
                                pe.wait_ge(a_ks, g + 1)
                                pe.wait_ge(a_qs, g + 1)
                            wait(pe, a_updr, n)
                            pe.matmul(bank[5][:, 0:E], ks[:, c, :], KV[:, c, 1, :], start=True, stop=True)\
                              .then_inc(a_upd, 1)
                            wait(pe, a_state, n)
                            if c == 0:
                                wait(pe, a_o, g)
                            pe.matmul(oc, S0[:, :], qs[:, c, :], start=True, stop=False)
                            pe.wait_ge(a_v, n + 1)
                        pe.wait_ge(a_mask, n * 4 + m + 1)
                        for h in range(4 * m, 4 * m + 4):
                            last = pe.matmul(oc, vpad[:, c % 2, h, :], probs[:, c % 2, h, :],
                                             start=False, stop=(h == H0 - 1))
                        if m == 3:
                            last.then_inc(a_attn, 1)

            def down(i, g, s):
                n = NPAIR[i] + 1
                pe.wait_ge(f_hl[i], g * n + s + 1)
                if s == 0 and (i == 1 or not (isinstance(g, int) and g == 0)):
                    pe.wait_ge(t_r, NG * (1 + 2 * i) + g)
                product(bank[6][:, :], w_hi[i][:, s, 2, :], w_lo[i][:, s, 2, :], h_hi[:, s % 3, :],
                        h_lo[:, s % 3, :], start=(s == 0), stop=(s == n - 1)).then_inc(f_d[i], 1)

            def main13(i, g, par, hook):
                n_pairs, stage = NPAIR[i], 1 + 2 * i
                n = n_pairs + 1
                x, x_rest = x_hi[:, par, :], x_lo[:, par, :]

                for u, (step, s, _) in enumerate(units_ffn(i)):
                    hook(u)
                    if u == 0:
                        if isinstance(g, int) and g == 0:
                            if i == 0:
                                pe.wait_ge(sel_ready, 2)
                                pe.wait_ge(a_mask, NG * NC * 4)
                                pe.wait_ge(a_o, NG)
                                pe.wait_ge(a_updr, NG * NC)
                            else:
                                pe.wait_ge(c_yT, NG * 8)
                                pe.wait_ge(c_u, NG * 12)
                                pe.wait_ge(c_mask, NG * 16)
                                pe.wait_ge(c_y, NG * NC)
                        pe.wait_ge(xl_ready, NG * (stage - 1) + g + 1)
                    if step == "gate":
                        if isinstance(g, int) and g == 0:
                            pe.wait_ge(f_wl[i], s + 1)
                        wait(pe, f_s[i], g * n + last_use(s, n, 2) + 1)
                        product(bank[s % 2][:, :], w_hi[i][:, s, 0, :], w_lo[i][:, s, 0, :], x, x_rest)\
                            .then_inc(f_g[i], 1)
                    elif step == "up":
                        wait(pe, f_t[i], g * n + last_use(s, n, 2) + 1)
                        product(bank[2 + s % 2][:, :], w_hi[i][:, s, 1, :], w_lo[i][:, s, 1, :], x, x_rest)\
                            .then_inc(f_u[i], 1)
                    elif step == "weight" and s < n_pairs:
                        if s == 0:
                            pe.wait_ge(t_cw, NG * i + g + 1)
                        wait(pe, f_h[i], g * n_pairs + last_use(s, n_pairs, 2) + 1)
                        pe.matmul(bank[4 + s % 2][:, :], sel[i][:, s, :], CW[:, cols(g)],
                                  start=True, stop=True).then_inc(f_w[i], 1)
                    elif step == "down" and s >= LAG:
                        down(i, g, s - LAG)

            def main2(g, par, hook):
                x, x_rest = x_hi[:, par, :], x_lo[:, par, :]

                def ring_wait(j):
                    k = j - RING
                    name, per_group, count = emptied(RING_JOBS[k])
                    wait(pe, c_empty[name], (g if k >= 0 else g - 1) * per_group + count)

                W = D2 + 1
                for u, (step, c, m) in enumerate(UNITS2):
                    hook(u)
                    n = g * NC + c
                    if u == 0:
                        if isinstance(g, int) and g == 0:
                            pe.wait_ge(d_w2, 64)
                            pe.wait_ge(init_s2, 3)
                            pe.wait_ge(f_s[0], NG * (NPAIR[0] + 1))
                            pe.wait_ge(f_t[0], NG * (NPAIR[0] + 1))
                            pe.wait_ge(f_h[0], NG * NPAIR[0])
                        pe.wait_ge(xl_ready, NG + g + 1)
                    if (step, c, m) in JOB:
                        j = JOB[(step, c, m)]
                        ring_wait(j)
                        b = bank[j % RING]
                    if step == "q":
                        if isinstance(g, int) and g == 0:
                            pe.wait_ge(c_wl, c // 4 + 1)
                        product(b[:, :], w2_hi[:, 0, c * P:(c + 1) * P], w2_lo[:, 0, c * P:(c + 1) * P], x, x_rest)\
                            .then_inc(c_filled, 1)
                    elif step == "kv":
                        if isinstance(g, int) and g == 0 and c == 0:
                            pe.wait_ge(c_wl, 2 + m + 1)
                        product(b[:, :], x[:, c * CH:(c + 1) * CH], x_rest[:, c * CH:(c + 1) * CH],
                                w_piece(w2_hi, 2 + m), w_piece(w2_lo, 2 + m)).then_inc(c_filled, 1)
                    elif step == "kT":
                        pe.wait_ge(c_comb, g * 16 + 8 + 2 * c + m + 1)
                        for t in range(4):
                            last = pe.transpose(b[:, t * P:(t + 1) * P],
                                                k2[:, c % 2, (4 * m + t) * P:(4 * m + t + 1) * P], ident)
                        last.then_inc(c_filled, 1)
                    elif step == "sc":
                        if m == 0:
                            pe.wait_ge(c_qb0, n + 1)
                            pe.wait_ge(c_qb1, n + 1)
                        pe.wait_ge(c_kT, g * 8 + 2 * c + m // 2 + 1)
                        for t in range(2):
                            last = pe.matmul(b[:, t * 2 * CH:(t + 1) * 2 * CH], kT2[:, 2 * m + t, :],
                                             qb2[:, c % 2, 2 * m + t, :, :], start=True, stop=True)
                        last.then_inc(c_filled, 1)
                    elif step == "num":
                        if m == 0:
                            wait(pe, c_y, n)
                            if c == 0:
                                pe.wait_ge(t_r, NG * 2 + g)
                            wait(pe, c_add, n)
                            pe.wait_ge(c_v, g * 8 + 2 * c + 2)
                            pe.wait_ge(c_mask, n * 4 + 4)
                        p0, p1 = UPAIRS[m]
                        for p in range(p0, p1):
                            o_ = (p - p0) * 2 * W
                            pe.matmul(bank[4 + m][:, o_:o_ + 2 * W], q2[:, p, c * CH:(c + 1) * CH],
                                      S2[:, p, :], start=True, stop=False)
                            for h in range(2):
                                last = pe.matmul(bank[4 + m][:, o_ + h * W:o_ + (h + 1) * W],
                                                 probs[:, c % 2, 2 * p + h, :], v2[:, c % 2, 2 * p + h, :],
                                                 start=False, stop=(h == 1))
                        last.then_inc(c_num, 1)
                    elif step == "U":
                        p0, p1 = UPAIRS[m]
                        for p in range(p0, p1):
                            o_ = (p - p0) * 2 * W
                            last = pe.matmul(b[:, o_:o_ + 2 * W], k2[:, c % 2, p * P:(p + 1) * P],
                                             v2[:, c % 2, 2 * p:2 * p + 2, :], start=True, stop=True)
                        last.then_inc(c_filled, 1)
                    elif step == "yT":
                        pe.wait_ge(c_y, n + 1)
                        for t in range(4):
                            q_ = 4 * m + t
                            last = pe.transpose(b[:, t * P:(t + 1) * P], y2[:, 2 * q_:2 * q_ + 2, :], ident)
                        last.then_inc(c_filled, 1)

            def main(stage, g, par, hook):
                if stage == 0:
                    main0(g, par, hook)
                elif stage == 2:
                    main2(g, par, hook)
                else:
                    main13(stage // 2, g, par, hook)

            def variance(sem_):
                for c in range(NC):
                    last = pe.matmul(T[:, c:c + 1], sq[:, c * CH:(c + 1) * CH], mean_w[:, 0:1], start=True, stop=True)
                last.then_inc(sem_, 1)

            def spread(sem_):
                for c in range(NC):
                    last = pe.matmul(T[:, c * CH:(c + 1) * CH], rstd[:, c:c + 1].to_broadcast([P, P]), ident,
                                     start=True, stop=True)
                last.then_inc(sem_, 1)

            def tail(stage, g, par, k):
                n, rn, i = tails(stage, g), routes(stage, g), stage // 2
                if k == "amean":
                    if isinstance(g, int) and g == 0:
                        pe.wait_ge(d_cst, 16)
                        pe.wait_ge(d_tail, 48)
                    wait(pe, t_cw, g)
                    pe.wait_ge(a_o, g + 1)
                    pe.matmul(T[:, :], mean_w, o, start=True, stop=True).then_inc(a_mean, 1)
                elif k == "avar":
                    pe.wait_ge(a_sq, g + 1)
                    variance(a_var)
                elif k == "abc":
                    pe.wait_ge(a_rs, g + 1)
                    spread(a_bc)
                elif k == "awo":
                    pe.wait_ge(a_og, g + 1)
                    pe.matmul(T[:, :], w0[:, 3, :], og, start=True, stop=True).then_inc(a_y, 1)
                elif k in ("d0", "d1", "d2"):
                    down(i, g, NPAIR[i] + 1 - LAG + int(k[1]))
                elif k in ("wo0", "wo1", "wo2", "wo3"):
                    m = int(k[2])
                    if m == 0:
                        pe.wait_ge(c_yT, g * 8 + 8)
                        pe.wait_ge(c_y, g * NC + NC)
                    for p in range(2 * m, 2 * m + 2):
                        last = pe.matmul(bank[6][:, :], w2o[:, p, :], yT2[:, p, :],
                                         start=(p == 0), stop=(p == PAIRS - 1))
                    if m == 3:
                        last.then_inc(c_y_out, 1)
                elif k == "mean":
                    pe.wait_ge(t_r, n + 1)
                    wait(pe, t_xo, n)
                    if stage:
                        wait(pe, t_cw, {1: NG, 2: g + NG, 3: 2 * NG}[stage])
                    pe.matmul(T[:, :], mean_w, r[:, :], start=True, stop=True).then_inc(t_mean, 1)
                elif k == "var":
                    pe.wait_ge(t_sq, n + 1)
                    variance(t_var)
                elif k == "bc":
                    pe.wait_ge(t_rs, n + 1)
                    spread(t_bc)
                elif k == "logit":
                    pe.wait_ge(t_xo, n + 1)
                    for c in range(NC):
                        last = pe.matmul(T[:, c * EXPERTS[i]:(c + 1) * EXPERTS[i]], xo[:, c * CH:(c + 1) * CH],
                                         w_route[i][:, :], start=True, stop=True)
                    last.then_inc(t_logit, 1)
                elif k == "cwT":
                    if stage == 0 and isinstance(g, int) and g == 0:
                        pe.wait_ge(ident_ready, 1)
                    pe.wait_ge(t_cwp, rn + 1)
                    for c in range(NC):
                        last = pe.transpose(T16[0:96, c * CH:(c + 1) * CH], parts[:, c, :, :], ident16[:, :])
                    last.then_inc(t_cwt, 1)

            schedule(pe, main, tail)

        @block.scalar
        def _(act):
            def split_x(stage, g, par):
                stage, g = following(stage, g)
                par = 1 - par
                if stage == 0 or stage == 4:
                    return
                act.wait_ge(*stored(stage - 1, g))
                old = isinstance(g, int) and g < 2
                gg, user = (g + NG - 2, stage - 1) if old else (g - 2, stage)
                if user == 0:
                    act.wait_ge(a_proj, gg * 6 + 6)
                elif user == 1 or user == 3:
                    act.wait_ge(f_u[user // 2], gg * (NPAIR[user // 2] + 1) + NPAIR[user // 2] + 1)
                elif user == 2:
                    act.wait_ge(c_filled, gg * JOBS + JOB[("kv", NC - 1, 3)] + 1)
                act.activation(x_hi[:, par, :], XT[:, cols(g)], ACT.Copy).then_inc(xh_ready, 1)

            def split_hidden(i, g, s):
                n = NPAIR[i] + 1
                if s < n - 1:
                    act.wait_ge(f_h[i], g * (n - 1) + s + 1)
                else:
                    act.wait_ge(f_t[i], g * n + n)
                wait(act, f_d[i], g * n + last_use(s, n, 3) + 1)
                act.activation(h_hi[:, s % 3, :], fh[s % 3], ACT.Copy).then_inc(f_hh[i], 1)

            def split_weights(i, s):
                act.activation(w_hi[i][:, s, :, :], w_f[i][:, s, :, :], ACT.Copy).then_inc(f_wh[i], 1)

            def main0(g, par, hook):
                for u, (step, _, _) in enumerate(UNITS0):
                    if u == X_AT[0] and isinstance(g, int) and g == 0:
                        act.activation(ident16[:, :], ident, ACT.Copy).then_inc(ident_ready, 1)
                        act.wait_ge(d_sel, 16)
                        for i, c0 in ((0, 0), (1, NPAIR[0] * P)):
                            act.activation(sel[i][:, :, :].rearrange("p s m -> p (s m)"),
                                           sel_stage[:, c0:c0 + NPAIR[i] * P], ACT.Copy).then_inc(sel_ready, 1)
                    if u == X_AT[0]:
                        split_x(0, g, par)
                    hook(u)
                    if step == "q":
                        pe_count, b, slot = 1, 0, 0
                        wait(act, a_kv, g * 2)
                    elif step == "k":
                        pe_count, b, slot = 2, 1, 1
                        wait(act, a_kz, g * 4)
                    elif step == "kv01":
                        pe_count, b, slot = 4, 3, 0
                        act.wait_ge(a_q, g + 1)
                    elif step == "kv23":
                        pe_count, b, slot = 6, 0, 0
                        act.wait_ge(a_kv, g * 2 + 1)
                    elif step == "g1":
                        act.wait_ge(a_proj, g * 6 + 3)
                        act.activation(g1[:, :], bank[2][:, :], ACT.Copy).then_inc(a_g1, 1)
                        continue
                    elif step == "gate":
                        act.wait_ge(a_proj, g * 6 + 5)
                        if not (isinstance(g, int) and g < 2):
                            act.wait_ge(a_og, g - 1)
                        act.activation(gate[:, par, :], bank[2][:, :], ACT.Sigmoid).then_inc(a_gate, 1)
                        continue
                    else:
                        continue
                    act.wait_ge(a_proj, g * 6 + pe_count)
                    act.activation(sig[:, slot, :], bank[b][:, :], ACT.Sigmoid).then_inc(a_sig, 1)
                    if step == "kv23":
                        if isinstance(g, int) and g == 0:
                            act.wait_ge(d_cst, 16)
                        act.wait_ge(a_k, g + 1)
                        wait(act, a_score, g * 16)
                        for q in range(4):
                            act.activation(kz[:, q, :], sig[:, 1, :], ACT.Copy,
                                           scale=cst[:, C_QUARTER + q:C_QUARTER + q + 1]).then_inc(a_kz, 1)

            def main13(i, g, par, hook):
                n = NPAIR[i] + 1
                first = isinstance(g, int) and g == 0
                for u, (step, s, _) in enumerate(units_ffn(i)):
                    if u == X_AT[1 + 2 * i]:
                        split_x(1 + 2 * i, g, par)
                    hook(u)
                    if u == 0 and first:
                        act.wait_ge(d_w13[i], 16)
                        if i == 0:
                            act.wait_ge(a_attn, NG * NC)
                        else:
                            act.wait_ge(c_num, NG * NC * 3)
                        split_weights(i, 0)
                        split_weights(i, 1)
                    if step != "gate":
                        continue
                    act.wait_ge(f_g[i], g * n + s + 1)
                    wait(act, f_t[i], g * n + last_use(s, n, 2) + 1)
                    act.activation(fs[:, s % 2, :], bank[s % 2][:, :], ACT.Silu).then_inc(f_s[i], 1)
                    if s >= 2:
                        split_hidden(i, g, s - 2)
                    if first and s + 2 < n:
                        split_weights(i, s + 2)

            def main2(g, par, hook):
                def relu_exp(b, m):
                    wait(act, c_comb, g * 16 + m - 1)
                    act.activation(relu2[:, m % 2, :], b[:, :], ACT.Relu)
                    act.activation(exp2[:, m % 2, :], b[:, :], ACT.Exp).then_inc(c_er, 1)

                first = isinstance(g, int) and g == 0
                for u, (step, c, m) in enumerate(UNITS2):
                    if u == X_AT[2]:
                        split_x(2, g, par)
                    hook(u)
                    if u == 0 and first:
                        act.wait_ge(d_w2, 64)
                        act.wait_ge(f_d[0], NG * (NPAIR[0] + 1))
                    if first:
                        for k in w_pieces_at(u, step, c):
                            act.activation(w_piece(w2_hi, k), w_piece(w2, k), ACT.Copy).then_inc(c_wh, 1)
                    if (step, c, m) in QB_AT:
                        d = QB_AT[(step, c, m)]
                        act.wait_ge(c_comb, g * 16 + 8)
                        wait(act, c_filled, qb_free(g, d))
                        act.activation(qb2[:, d % 2, :, 0, :], q2[:, :, d * CH:(d + 1) * CH], ACT.Copy,
                                       scale=cst[:, C_HALF:C_HALF + 1]).then_inc(c_qb0, 1)
                    if step not in ("q", "kv", "yT", "U"):
                        continue
                    j = JOB[(step, c, m)]
                    b = bank[j % RING]
                    act.wait_ge(c_filled, g * JOBS + j + 1)
                    if step == "q":
                        relu_exp(b, c)
                    elif step == "kv" and m < 2:
                        relu_exp(b, 8 + 2 * c + m)
                    elif step == "kv":
                        h0 = 8 * (m - 2)
                        act.activation(v2[:, c % 2, h0:h0 + 8, 0:D2], b[:, :].rearrange("p (h d) -> p h d", d=D2),
                                       ACT.Copy).then_inc(c_v, 1)
                    elif step == "U":
                        p0, p1 = UPAIRS[m]
                        if m == 0:
                            wait(act, c_add, g * NC + c)
                        act.activation(u2[:, p0:p1, :],
                                       b[:, 0:(p1 - p0) * 2 * (D2 + 1)].rearrange("p (q w) -> p q w", q=p1 - p0),
                                       ACT.Copy).then_inc(c_u, 1)
                    else:
                        act.activation(yT2[:, 4 * m:4 * m + 4, c * CH:(c + 1) * CH],
                                       b[:, :].rearrange("p (q t) -> p q t", q=4), ACT.Copy).then_inc(c_yT, 1)

            def main(stage, g, par, hook):
                if stage == 0:
                    main0(g, par, hook)
                elif stage == 2:
                    main2(g, par, hook)
                else:
                    main13(stage // 2, g, par, hook)

            def tail(stage, g, par, k):
                n, rn, i = tails(stage, g), routes(stage, g), stage // 2
                if k in ("h1", "h2"):
                    split_hidden(i, g, NPAIR[i] - 2 + int(k[1]))
                elif k == "asq":
                    act.wait_ge(a_c, g + 1)
                    act.activation(sq[:, :], r[:, :], ACT.Square).then_inc(a_sq, 1)
                elif k == "sq":
                    act.wait_ge(t_c, n + 1)
                    act.activation(sq[:, :], r[:, :], ACT.Square).then_inc(t_sq, 1)
                elif k == "sig":
                    act.wait_ge(t_logit, rn + 1)
                    wait(act, t_cwp, rn)
                    act.activation(sg[i][:, :, :, 0:EXPERTS[i] // RG],
                                   T[:, 0:NC * EXPERTS[i]].rearrange("p (c g k) -> p c g k", c=NC, g=RG),
                                   ACT.Exp if i else ACT.Sigmoid, scale=-1.0 if i else 1.0).then_inc(t_sig, 1)
                elif k == "cw":
                    act.wait_ge(t_cwt, rn + 1)
                    act.activation(CW[:, cols(g)], T16[0:96, 0:GROUP], ACT.Copy).then_inc(t_cw, 1)

            schedule(act, main, tail)

        @block.vector
        def _(dve):
            def main0(g, par, hook):
                for u, (step, c, m) in enumerate(UNITS0):
                    hook(u)
                    n = g * NC + c
                    if step == "q":
                        dve.wait_ge(a_sig, g * 4 + 1)
                        wait(dve, a_attn, g * NC)
                        wait(dve, a_qs, g)
                        wait(dve, a_qbd, g)
                        dve.tensor_tensor(qT[:, :, :].rearrange("p c t -> p (c t)"), bank[0][:, :], sig[:, 0, :],
                                          ALU.mult).then_inc(a_q, 1)
                    elif step == "k":
                        dve.wait_ge(a_sig, g * 4 + 2)
                        dve.tensor_tensor(sig[:, 1, :], bank[1][:, :], sig[:, 1, :], ALU.mult).then_inc(a_k, 1)
                    elif step == "g1":
                        if isinstance(g, int) and g == 0:
                            dve.wait_ge(d_cst, 16)
                        dve.wait_ge(a_q, g + 1)
                        for h in range(4):
                            last = dve.tensor_scalar(qbd[:, :, h, :], qT[:, :, :], cst[:, C_HEAD + h:C_HEAD + h + 1],
                                                     None, ALU.mult)
                        last.then_inc(a_qbd, 1)
                    elif step in ("kv01", "kv23"):
                        m = 0 if step == "kv01" else 1
                        dve.wait_ge(a_sig, g * 4 + 3 + m)
                        wait(dve, a_v, g * NC)
                        wait(dve, a_ks, g)
                        dve.tensor_tensor(KV[:, 2 * m:2 * m + 2, :, :].rearrange("p c k e -> p (c k e)"),
                                          bank[3 if m == 0 else 0][:, :], sig[:, 0, :], ALU.mult).then_inc(a_kv, 1)
                    elif step == "sc":
                        if m == 0:
                            wait(dve, a_attn, n - 1)
                        if isinstance(g, int) and n == 0 and m == 0:
                            dve.wait_ge(d_mask, 16)
                        dve.wait_ge(a_score, n * 4 + m + 1)
                        dve.tensor_tensor(probs[:, c % 2, 4 * m:4 * m + 4, :],
                                          bank[m][:, :].rearrange("p (h t) -> p h t", h=4),
                                          mask0[:, 4 * m:4 * m + 4, :], ALU.mult).then_inc(a_mask, 1)
                    elif step == "pv" and m == 2:
                        dve.wait_ge(a_upd, n + 1)
                        wait(dve, a_state, n)
                        dve.tensor_tensor(upd[:, :], bank[5][:, 0:E], block0, ALU.mult).then_inc(a_updr, 1)
                    elif step == "pv" and m == 3:
                        dve.wait_ge(a_updr, n + 1)
                        dve.wait_ge(a_attn, n + 1)
                        if par == 1 and c == NC - 1:
                            dve.memset(S0[:, :], 0.0).then_inc(a_state, 1)
                        else:
                            dve.scalar_tensor_tensor(out=S0[:, :], in0=S0[:, :], scalar=lamc, in1=upd[:, :],
                                                     op0=ALU.mult, op1=ALU.add).then_inc(a_state, 1)

            def main13(i, g, par, hook):
                n_pairs = NPAIR[i]
                n = n_pairs + 1

                def weigh(s):
                    dve.wait_ge(f_w[i], g * n_pairs + s + 1)
                    dve.wait_ge(f_t[i], g * n + s + 1)
                    wait(dve, f_hl[i], g * n + last_use(s, n, 3) + 1)
                    dve.tensor_tensor(fh[s % 3], ft[:, s % 2, :], bank[4 + s % 2][:, :],
                                      ALU.mult).then_inc(f_h[i], 1)

                def split_weights(s):
                    dve.wait_ge(f_wh[i], s + 1)
                    dve.tensor_tensor(w_lo[i][:, s, :, :], w_f[i][:, s, :, :], w_hi[i][:, s, :, :].bitcast(F32),
                                      ALU.subtract).then_inc(f_wl[i], 1)

                first = isinstance(g, int) and g == 0
                for u, (step, s, _) in enumerate(units_ffn(i)):
                    hook(u)
                    if u == 0 and first:
                        split_weights(0)
                        split_weights(1)
                    if step == "down" and 1 <= s < n_pairs:
                        weigh(s - 1)
                    if step != "weight":
                        continue
                    if s == n_pairs:
                        weigh(s - 1)
                    dve.wait_ge(f_s[i], g * n + s + 1)
                    dve.wait_ge(f_u[i], g * n + s + 1)
                    dst = ft[:, s % 2, :]
                    wait(dve, f_h[i], g * n_pairs + (s - 1 if s >= 2 else 0))
                    if s == n_pairs:
                        dst = fh[s % 3]
                        wait(dve, f_hl[i], g * n + last_use(s, n, 3) + 1)
                    dve.tensor_tensor(dst, fs[:, s % 2, :], bank[2 + s % 2][:, :], ALU.mult).then_inc(f_t[i], 1)
                    if first and s + 2 < n:
                        split_weights(s + 2)

            def main2(g, par, hook):
                W = D2 + 1

                def combine(dst, m):
                    dve.wait_ge(c_er, g * 16 + m + 1)
                    dve.scalar_tensor_tensor(out=dst, in0=exp2[:, m % 2, :], scalar=1.0, in1=relu2[:, m % 2, :],
                                             op0=ALU.min, op1=ALU.add).then_inc(c_comb, 1)

                for u, (step, c, m) in enumerate(UNITS2):
                    hook(u)
                    if isinstance(g, int) and g == 0:
                        for k in w_pieces_at(u, step, c):
                            dve.wait_ge(c_wh, k + 1)
                            dve.tensor_tensor(w_piece(w2_lo, k), w_piece(w2, k), w_piece(w2_hi, k).bitcast(F32),
                                              ALU.subtract).then_inc(c_wl, 1)
                    n = g * NC + c
                    j = JOB.get((step, c, m))
                    if step == "q":
                        if c == 0:
                            wait(dve, c_num, g * NC * 3)
                            wait(dve, c_qb0, g * NC)
                            wait(dve, c_qb1, g * NC)
                        combine(q2[:, c, :], c)
                    elif step == "kv" and m < 2:
                        combine(k2[:, c % 2, m * 512:(m + 1) * 512], 8 + 2 * c + m)
                    elif step == "kT":
                        dve.wait_ge(c_filled, g * JOBS + j + 1)
                        dve.tensor_copy(kT2[:, 4 * m:4 * m + 4, :],
                                        bank[j % RING][:, :].rearrange("p (q t) -> p q t", q=4)).then_inc(c_kT, 1)
                    elif step == "sc":
                        if m == 0:
                            wait(dve, c_num, 3 * (n - 1))
                        dve.wait_ge(c_filled, g * JOBS + j + 1)
                        dve.tensor_tensor(probs[:, c % 2, 4 * m:4 * m + 4, :],
                                          bank[j % RING][:, :].rearrange("p (h t) -> p h t", h=4),
                                          tri[:, None, :].to_broadcast([P, 4, CH]), ALU.mult).then_inc(c_mask, 1)
                    elif step == "num":
                        p0, p1 = UPAIRS[m]
                        v = bank[4 + m][:, 0:(p1 - p0) * 2 * W].rearrange("p (h w) -> p h w", w=W)
                        at = 6 * n + 2 * m
                        dve.wait_ge(c_num, 3 * n + m + 1)
                        dve.tensor_scalar(den2[:, 0, 2 * p0:2 * p1], v[:, :, D2], 1e-6, None,
                                          ALU.add).then_inc(c_den, 1)
                        dve.wait_ge(c_den, at + 1)
                        dve.reciprocal(den2[:, 1, 2 * p0:2 * p1], den2[:, 0, 2 * p0:2 * p1]).then_inc(c_den, 1)
                        dve.wait_ge(c_den, at + 2)
                        if m == 0 and c == 0:
                            wait(dve, c_filled, g * JOBS - JOBS + JOB[("yT", NC - 1, 1)] + 1)
                        elif m == 0:
                            dve.wait_ge(c_filled, g * JOBS + JOB[("yT", c - 1, 1)] + 1)
                        last = dve.tensor_tensor(y2[:, 2 * p0:2 * p1, :], v[:, :, 0:D2],
                                                 den2[:, 1, 2 * p0:2 * p1, None].to_broadcast([P, 2 * (p1 - p0), D2]),
                                                 ALU.mult)
                        if m < 2:
                            continue
                        last.then_inc(c_y, 1)
                        if par == 1 and c == NC - 1:
                            dve.memset(S2[:, :, :], 0.0).then_inc(c_add, 1)
                        else:
                            dve.wait_ge(c_u, 3 * n + 3)
                            for h in range(2):
                                rows, w_ = slice(64 * h, 64 * h + 64), slice(h * W, (h + 1) * W)
                                last = dve.tensor_tensor(S2[rows, :, w_], S2[rows, :, w_], u2[rows, :, w_], ALU.add)
                            last.then_inc(c_add, 1)

            def main(stage, g, par, hook):
                if stage == 0:
                    main0(g, par, hook)
                elif stage == 2:
                    main2(g, par, hook)
                else:
                    main13(stage // 2, g, par, hook)

            def route(i, rn, part):
                at = [0]
                before = (rn - NG * i) * sum(ROUTE_OPS[i]) + NG * i * sum(ROUTE_OPS[0]) + sum(ROUTE_OPS[i][:part])

                def then(ins):
                    at[0] += 1
                    ins.then_inc(route_step, 1)
                    wait_apart(dve, route_step, before + at[0], passed_dve)

                sgi = sg[i][:, :, :, :].rearrange("p c g k -> p c (g k)")
                ch_t = ch[:, :, :].rearrange("p (c g) k -> p c (g k)", c=NC)
                shape = [P, NC, RG, RG]
                if part == 0:
                    dve.wait_ge(t_sig, rn + 1)
                    wait(dve, t_cwt, rn)
                    wait(dve, t_cwp, rn)
                    if i == 1:
                        some = sg[i][:, :, :, 0:EXPERTS[i] // RG]
                        then(dve.tensor_scalar(some, some, 1.0, None, ALU.add))
                        then(dve.reciprocal(some, some))
                    then(dve.tensor_tensor(ch_t, sgi, rbias[i][:, None, :].to_broadcast([P, NC, RW]), ALU.add))
                    for n in range(NC * RG):
                        last = dve.max(top8[:, n, :], ch[:, n, :])
                    then(last)
                elif part == 1:
                    gsf = gs[:, :, :].rearrange("p c g -> p (c g)")
                    then(dve.tensor_tensor(gsf, top8[:, :, 0], top8[:, :, 1], ALU.add))
                    other, own = gs[:, :, None, :].to_broadcast(shape), gs[:, :, :, None].to_broadcast(shape)
                    dve.tensor_tensor(ge[:, :, :, :], other, own, ALU.is_ge)
                    then(dve.tensor_tensor(gt[:, :, :, :], other, own, ALU.is_gt))
                    dve.tensor_tensor(ge[:, :, :, :], ge[:, :, :, :], lower[:, None, :, :].to_broadcast(shape),
                                      ALU.mult)
                    then(dve.tensor_tensor(gt[:, :, :, :], gt[:, :, :, :], upper[:, None, :, :].to_broadcast(shape),
                                           ALU.mult))
                elif part == 2:
                    then(dve.tensor_tensor(ge[:, :, :, :], ge[:, :, :, :], gt[:, :, :, :], ALU.add))
                    then(dve.tensor_reduce(rank[:, :], ge[:, :, :, :].rearrange("p c i j -> p (c i) j"), AX.X, ALU.add))
                    then(dve.tensor_scalar(rank[:, :], rank[:, :], 1.5, None, ALU.is_lt))
                elif part == 3:
                    if i == 1:
                        then(dve.tensor_scalar(fill[:, :], rank[:, :], -1.0, OUT_OF_GROUP, ALU.add, ALU.mult))
                    kept = rank[:, :, None].to_broadcast([P, NC * RG, 8])
                    then(dve.tensor_tensor(ch[:, :, :], ch[:, :, :], kept, ALU.mult))
                    if i == 1:
                        then(dve.tensor_tensor(ch[:, :, :], ch[:, :, :], fill[:, :, None].to_broadcast([P, NC * RG, 8]),
                                               ALU.add))
                elif part == 4:
                    for c in range(NC):
                        last = dve.max(top[:, c, :], ch_t[:, c, :])
                    then(last)
                    if i == 1:
                        then(dve.memset(top[:, :, 4:8], PAD))
                elif part == 5:
                    for c in range(NC):
                        last = dve.match_replace(mr[:, c, :], top[:, c, :], ch_t[:, c, :], TAKEN)
                    then(last)
                elif part == 6:
                    then(dve.tensor_tensor(mr[:, :, :], mr[:, :, :], ch_t, ALU.not_equal))
                    then(dve.tensor_tensor(cw[:, :, :], mr[:, :, :], sgi, ALU.mult))
                    then(dve.tensor_reduce(wsum[:, :], cw[:, :, :], AX.X, ALU.add))
                elif part == 7:
                    then(dve.tensor_scalar(wsum[:, :], wsum[:, :], 1e-20, None, ALU.add))
                    then(dve.reciprocal(wsum[:, :], wsum[:, :]))
                    then(dve.scalar_tensor_tensor(out=cw[:, :, :], in0=cw[:, :, :], scalar=SCALE,
                                                  in1=wsum[:, :, None].to_broadcast([P, NC, RW]),
                                                  op0=ALU.mult, op1=ALU.mult))
                else:
                    then(dve.tensor_copy(parts[:, :, 0, :], cw[:, :, :]))
                    then(dve.tensor_tensor(cw[:, :, :], cw[:, :, :], parts[:, :, 0, :], ALU.subtract))
                    then(dve.tensor_copy(parts[:, :, 1, :], cw[:, :, :]))
                    then(dve.tensor_tensor(mr[:, :, :], cw[:, :, :], parts[:, :, 1, :], ALU.subtract))
                    dve.tensor_copy(parts[:, :, 2, :], mr[:, :, :]).then_inc(t_cwp, 1)
                assert at[0] == ROUTE_OPS[i][part]

            def tail(stage, g, par, k):
                n, rn, i = tails(stage, g), routes(stage, g), stage // 2
                if k == "o":
                    dve.wait_ge(a_attn, g * NC + NC)
                    wait(dve, a_mean, g)
                    wait(dve, a_c, g)
                    dve.tensor_copy(o, bank[4][:, :]).then_inc(a_o, 1)
                elif k == "ac":
                    dve.wait_ge(a_mean, g + 1)
                    dve.wait_ge(a_o, g + 1)
                    wait(dve, t_xo, n)
                    dve.tensor_tensor(r[:, :], o, T[:, :], ALU.subtract).then_inc(a_c, 1)
                elif k == "ave":
                    dve.wait_ge(a_var, g + 1)
                    dve.tensor_scalar(var[:, :], T[:, 0:NC], 1e-5, None, ALU.add).then_inc(a_ve, 1)
                elif k == "an":
                    dve.wait_ge(a_bc, g + 1)
                    dve.tensor_tensor(og, r[:, :], T[:, :], ALU.mult).then_inc(a_n, 1)
                elif k == "agb":
                    dve.wait_ge(a_n, g + 1)
                    dve.tensor_scalar(ogb[:, :], og, gb[:, 0:1], gb[:, 1:2], ALU.mult, ALU.add).then_inc(a_gb, 1)
                elif k == "aog":
                    dve.wait_ge(a_gb, g + 1)
                    dve.wait_ge(a_gate, g + 1)
                    dve.tensor_tensor(og, ogb[:, :], gate[:, par, :], ALU.mult).then_inc(a_og, 1)
                elif k == "r":
                    if stage == 0:
                        dve.wait_ge(a_y, g + 1)
                    elif stage == 2:
                        dve.wait_ge(c_y_out, g + 1)
                    else:
                        dve.wait_ge(f_d[i], (g + 1) * (NPAIR[i] + 1))
                    if stage:
                        dve.wait_ge(*stored(stage - 1, g))
                    wait(dve, t_xo, n)
                    y = {0: T, 1: bank[6], 2: bank[6], 3: bank[6]}[stage]
                    dve.scalar_tensor_tensor(out=r[:, :], in0=XT[:, cols(g)], scalar=2.0 if stage == 3 else 1.0,
                                             in1=y[:, :], op0=ALU.mult, op1=ALU.add).then_inc(t_r, 1)
                elif k == "c":
                    dve.wait_ge(t_mean, n + 1)
                    dve.wait_ge(t_r, n + 1)
                    dve.tensor_tensor(r[:, :], r[:, :], T[:, :], ALU.subtract).then_inc(t_c, 1)
                elif k == "ve":
                    dve.wait_ge(t_var, n + 1)
                    dve.tensor_scalar(var[:, :], T[:, 0:NC], 1e-5, None, ALU.add).then_inc(t_ve, 1)
                elif k == "xo":
                    dve.wait_ge(t_bc, n + 1)
                    if stage % 2:
                        dst = XT[:, cols(g)]
                    else:
                        dst = xo[:, :]
                        wait(dve, xt_ready, rn)
                    dve.tensor_tensor(dst, r[:, :], T[:, :], ALU.mult).then_inc(t_xo, 1)
                elif isinstance(k, int):
                    route(i, rn, k)

            dve.memset(vpad, 0.0).then_inc(init_v, 1)
            dve.memset(S0[:, :], 0.0).then_inc(init_v, 1)
            dve.wait_ge(init_v, 2)
            schedule(dve, main, tail)

        @block.gpsimd
        def _(pool):
            def split_x(stage, g, par):
                stage, g = following(stage, g)
                par = 1 - par
                if stage == 4:
                    return
                if stage == 0:
                    copy_x(g, par)
                    return
                wait_apart(pool, xh_ready, NG * (stage - 1) + g + 1, passed_pool)
                pool.tensor_tensor(x_lo[:, par, :], XT[:, cols(g)], x_hi[:, par, :].bitcast(F32),
                                   ALU.subtract).then_inc(xl_ready, 1)

            def split_hidden(i, g, s):
                wait_apart(pool, f_hh[i], g * (NPAIR[i] + 1) + s + 1, passed_pool)
                pool.tensor_tensor(h_lo[:, s % 3, :], fh[s % 3], h_hi[:, s % 3, :].bitcast(F32),
                                   ALU.subtract).then_inc(f_hl[i], 1)

            def copy_x(g, par):
                if isinstance(g, int) and g == 1:
                    pool.wait_ge(d_x, 16)
                if not (isinstance(g, int) and g < 2):
                    wait_apart(pool, a_proj, g * 6 - 6, passed_pool)
                pool.tensor_copy(x_group[:, par, :], XT[:, cols(g)]).then_inc(x_ready, 1)

            def main0(g, par, hook):
                for u, (step, c, m) in enumerate(UNITS0):
                    if u == X_AT[0]:
                        split_x(0, g, par)
                    hook(u)
                    n = g * NC + c
                    if step == "k":
                        if isinstance(g, int) and g == 0:
                            pool.wait_ge(d_cst, 16)
                        wait_apart(pool, a_q, g + 1, passed_pool)
                        pool.tensor_tensor(qs[:, :, :], qT[:, :, :], lamq[:, None, :].to_broadcast([P, NC, CH]),
                                           ALU.mult).then_inc(a_qs, 1)
                    elif step == "kv23":
                        wait_apart(pool, a_kv, g * 2 + 2, passed_pool)
                        pool.tensor_tensor(ks[:, :, :], KV[:, :, 0, :], lamk[:, None, :].to_broadcast([P, NC, E]),
                                           ALU.mult).then_inc(a_ks, 1)
                    elif step == "sc" and m == 0:
                        wait_apart(pool, a_attn, n - 1, passed_pool)
                        dst = vpad[:, c % 2, :, :].rearrange("p h e -> p (h e)")
                        v = KV[:, c, 1, :]
                        most = H0 - 1
                        pool.tensor_copy(dst[:, 0:most * (E + D0)].rearrange("p (h w) -> p h w", h=most)[:, :, 0:D0],
                                         v[:, 0:most * D0].rearrange("p (h d) -> p h d", h=most))
                        pool.tensor_copy(dst[:, most * (E + D0):], v[:, most * D0:]).then_inc(a_v, 1)

            def main13(stage, g, par, hook):
                for u, (step, s, _) in enumerate(UNITS[stage]):
                    if u == X_AT[stage]:
                        split_x(stage, g, par)
                    hook(u)
                    if step == "gate" and s >= 2:
                        split_hidden(stage // 2, g, s - 2)

            def main2(g, par, hook):
                for u, (step, c, m) in enumerate(UNITS2):
                    if u == X_AT[2]:
                        split_x(2, g, par)
                    hook(u)
                    if (step, c, m) in QB_AT:
                        c = QB_AT[(step, c, m)]
                        wait_apart(pool, c_comb, g * 16 + 8, passed_pool)
                        wait_apart(pool, c_filled, qb_free(g, c), passed_pool)
                        pool.tensor_scalar(qb2[:, c % 2, :, 1, :], q2[:, :, c * CH:(c + 1) * CH],
                                           cst[:, C_HALF + 1:C_HALF + 2], 0.0, ALU.mult, ALU.add).then_inc(c_qb1, 1)

            def main(stage, g, par, hook):
                if stage == 0:
                    main0(g, par, hook)
                elif stage == 2:
                    main2(g, par, hook)
                else:
                    main13(stage, g, par, hook)

            def tail(stage, g, par, k):
                n, i = tails(stage, g), stage // 2
                if k in ("h1", "h2"):
                    split_hidden(i, g, NPAIR[i] - 2 + int(k[1]))
                elif k == "apow":
                    wait_apart(pool, a_ve, g + 1, passed_pool)
                    pool.tensor_tensor(rstd[:, :], var[:, :], minus_half[:, :], ALU.pow).then_inc(a_rs, 1)
                elif k == "pow":
                    wait_apart(pool, t_ve, n + 1, passed_pool)
                    pool.tensor_tensor(rstd[:, :], var[:, :], minus_half[:, :], ALU.pow).then_inc(t_rs, 1)
                elif k == "xt":
                    wait_apart(pool, t_xo, n + 1, passed_pool)
                    pool.tensor_copy(XT[:, cols(g)], xo[:, :]).then_inc(xt_ready, 1)

            pool.memset(w0[:, 4:6, :], 0.0).then_inc(init_pool, 1)
            pool.memset(rbias[1][:, :], PAD).then_inc(init_pool, 1)
            pool.memset(minus_half[:, :], -0.5).then_inc(init_half, 1)
            pool.wait_ge(init_half, 1)
            pool.memset(sg[1][:, :, :, :], 0.0).then_inc(init_s2, 1)
            pool.memset(v2[:, :, :, :], 1.0).then_inc(init_s2, 1)
            pool.memset(S2[:, :, :], 0.0).then_inc(init_s2, 1)
            schedule(pool, main, tail)


def constants():
    start = 2.0 ** (-2.0 ** (-(np.log2(H0) - 3)))
    slopes = np.array([start * start ** i for i in range(H0)], np.float32) * np.float32(1.0 + 1e-05)
    s = slopes.astype(np.float64)
    t = np.arange(CH)
    diff = t[None, :] - t[:, None]
    c = np.zeros((P, C_END), np.float32)
    mask = np.where(diff[:, None, :] >= 0, np.exp(-s[None, :, None] * np.maximum(diff, 0)[:, None, :]), 0.0)
    c[:, C_MASK0:C_LAMQ] = mask.reshape(P, -1)
    head = np.arange(E) // D0
    c[:, C_LAMQ:C_LAMK] = np.exp(-s[head][:, None] * (t[None, :] + 1.0))
    c[:, C_LAMK:C_BLOCK] = np.exp(-s[head][None, :] * (CH - 1.0 - t[:, None]))
    c[:, C_BLOCK:C_TRI] = head[:, None] == head[None, :]
    c[:, C_TRI:C_IDENT] = diff >= 0
    c[:, C_IDENT:C_MEAN] = np.eye(P)
    c[:, C_MEAN:C_HEAD] = 1.0 / E
    c[:, C_HEAD:C_LOWER] = (head % 4)[:, None] == np.arange(4)[None, :]
    i, j = np.arange(RG)[:, None], np.arange(RG)[None, :]
    c[:, C_LOWER:C_UPPER] = (j < i).reshape(-1)
    c[:, C_UPPER:C_LAMC] = (j > i).reshape(-1)
    c[:, C_LAMC] = np.exp(-s[head] * CH)
    c[:, C_QUARTER:C_END] = (np.arange(P) // 32)[:, None] == np.arange(4)[None, :]
    c[:, C_HALF:C_QUARTER] = (np.arange(P) // D2)[:, None] == np.arange(2)[None, :]
    rows = np.zeros((3, RW, NPAIR[0] + NPAIR[1], P), np.float32)
    at = 0
    for n in EXPERTS:
        for e in range(n):
            col = (e // (n // RG)) * 8 + e % (n // RG)
            rows[:, col, at + e // 2, (e % 2) * INNER:(e % 2 + 1) * INNER] = 1.0
        at += n // 2
    return c, rows.reshape(96, -1)


def arrange(inputs):
    z = {k: np.asarray(v) for k, v in inputs.items()}
    cst, sel = constants()
    d = {"cst": cst, "sel": sel, "x": z["L0_attn_x"].reshape(TOK, E).T}
    d["aW"] = np.stack([z["L0_attn_" + n] for n in ("Wq", "Wk", "Wv", "Wo")], 1)
    d["aWg1"], d["aWg2"] = z["L0_attn_Wg1"], z["L0_attn_Wg2"]
    d["gb"] = np.stack([z["L0_attn_gamma"].reshape(E), z["L0_attn_beta"].reshape(E)], 1)
    experts = (("L0_ffn_expert_gate", "L0_ffn_expert_up", "L0_ffn_expert_down",
                "L0_ffn_shared_gate", "L0_ffn_shared_up", "L0_ffn_shared_down"),
               ("L1_ffn_Wg", "L1_ffn_Wu", "L1_ffn_Wd", "L1_ffn_Ws_g", "L1_ffn_Ws_u", "L1_ffn_Ws_d"))
    for i, (g, u, w, sg, su, sd) in enumerate(experts):
        n = NPAIR[i]
        gu = [np.concatenate([z[m].reshape(n, P, E), z[s].reshape(1, P, E)]).transpose(2, 0, 1)
              for m, s in ((g, sg), (u, su))]
        down = np.concatenate([z[w].transpose(0, 2, 1).reshape(n, P, E), z[sd].T.reshape(1, P, E)])
        d[f"w{i}"] = np.stack([gu[0], gu[1], down.transpose(1, 0, 2)], 2)
    d["gw1"], d["gw3"] = z["L0_ffn_gate_w"].T, z["L1_ffn_gate_w"].T
    d["gb1"] = np.broadcast_to(z["L0_ffn_gate_bias"], (P, EXPERTS[0]))
    d["gb3"] = np.broadcast_to(z["L1_ffn_gate_bias"], (P, EXPERTS[1]))
    d["w2"] = np.stack([z["L1_attn_" + n] for n in ("Wq", "Wk", "Wv")], 1)
    d["w2o"] = z["L1_attn_Wo"].reshape(PAIRS, P, E).transpose(1, 0, 2)
    return {k: np.ascontiguousarray(v) for k, v in d.items()}


def kernel(**inputs):
    import concourse.bacc as bacc
    from concourse.bass_utils import run_bass_kernel_spmd

    nc = bacc.Bacc("TRN2", target_bir_lowering=False, num_devices=1)
    data = arrange(inputs)
    arrays = {f"in_{k}": v for k, v in data.items()}
    handles = {k: nc.dram_tensor(f"in_{k}", v.shape, mybir.dt.from_np(v.dtype), kind="ExternalInput").ap()
               for k, v in data.items()}
    out = nc.dram_tensor("out", (E, TOK), F32, kind="ExternalOutput").ap()
    build(nc, handles, out)
    got = run_bass_kernel_spmd(nc, [arrays], core_ids=[0]).results[0]["out"]
    return np.ascontiguousarray(got.T).reshape(BATCH, SEQ, E)
```
